# Optimizing a Trainium2 kernel written in Bass

```python
import numpy as np
import jax
import jax.numpy as jnp

def _softmax(x, axis=-1):
    return jax.nn.softmax(x, axis=axis)
def _gelu(x):
    return jax.nn.gelu(x, approximate=True)
def _silu(x):
    return jax.nn.silu(x)
def _sigmoid(x):
    return jax.nn.sigmoid(x)
def _layernorm(x, axis=-1, eps=1e-5):
    m = jnp.mean(x, axis=axis, keepdims=True)
    v = jnp.var(x, axis=axis, keepdims=True)
    return (x - m) / jnp.sqrt(v + eps)
def _scatter_add(tgt, idx, src, axis=0):
    return tgt.at[idx].add(src)
def _segment_sum(src, seg, n):
    return jax.ops.segment_sum(src, seg, n)

kernel_name = 'mk_adj_preln_d1_adj_128_b6e813'

def setup_inputs(seed: int = 0):
    np.random.seed(seed)
    _w = jnp.asarray
    def _rec_inputs():
        import jax
        import jax.numpy as jnp
        _gk = jax.random.key(seed)
        x = -9.806e-05 + 1 * jax.random.normal(jax.random.fold_in(_gk, 1), (8192, 128), jnp.float32)
        _a = jax.random.bernoulli(jax.random.fold_in(_gk, 2), 0.000976562, (8192, 8192))
        _a = jnp.logical_or(_a, jnp.swapaxes(_a, -1, -2))
        _a = jnp.logical_or(_a, jnp.eye(8192, dtype=bool))
        _af = _a.astype(jnp.float32)
        _af = _af * jax.random.uniform(jax.random.fold_in(_gk, 3), (8192, 8192), jnp.float32, 0.05, 1)
        adj = _af
        return x, adj
    x, adj = _rec_inputs()
    def _L0_gnn_setup():
        import jax, jax.numpy as jnp
        import numpy as np

        def _lap_mul(A, x):
            d = 1.0 / jnp.sqrt(jnp.sum(A, axis=-1))
            return d[:, None] * (A @ (d[:, None] * x))
        key = jax.random.key(seed)
        k1, k2, k3, k4, k5, k6 = jax.random.split(key, 6)
        N, D_IN, D_OUT = (4096, 128, 128)
        x = jax.random.normal(k1, (N, D_IN), dtype=jnp.float32)
        A = jax.random.uniform(k2, (N, N), dtype=jnp.float32)
        s1 = 1.0 / np.sqrt(D_IN)
        W1 = jax.random.uniform(k3, (D_IN, D_OUT), minval=-s1, maxval=s1, dtype=jnp.float32)
        b1 = jax.random.uniform(k4, (D_OUT,), minval=-s1, maxval=s1, dtype=jnp.float32)
        W2 = jax.random.uniform(k5, (D_IN, D_OUT), minval=-s1, maxval=s1, dtype=jnp.float32)
        b2 = jax.random.uniform(k6, (D_OUT,), minval=-s1, maxval=s1, dtype=jnp.float32)
        return {'x': x, 'A': A, 'W1': W1, 'b1': b1, 'W2': W2, 'b2': b2, 'sigma': 1, 'k': 4}
    _L0_gnn_all = _L0_gnn_setup()
    _L0_gnn_in = {k: v for k, v in _L0_gnn_all.items() if k in ('W1', 'b1', 'W2', 'b2', )}
    del _L0_gnn_all

    return {
        "x": x,
        "adj": adj,
        "L0_gnn_W1": _L0_gnn_in["W1"],
        "L0_gnn_b1": _L0_gnn_in["b1"],
        "L0_gnn_W2": _L0_gnn_in["W2"],
        "L0_gnn_b2": _L0_gnn_in["b2"],
    }

def reference(x, adj, L0_gnn_W1, L0_gnn_b1, L0_gnn_W2, L0_gnn_b2):
    import jax
    import jax.numpy as jnp
    def _L0_gnn_ref(x, A, W1, b1, W2, b2, sigma, k):
        import jax, jax.numpy as jnp
        import numpy as np

        def _lap_mul(A, x):
            d = 1.0 / jnp.sqrt(jnp.sum(A, axis=-1))
            return d[:, None] * (A @ (d[:, None] * x))
        z = _lap_mul(A, x) @ W1 + b1
        z = jax.nn.leaky_relu(z, negative_slope=0.1)
        sq = jnp.sum(z * z, axis=-1)
        d2 = sq[:, None] + sq[None, :] - 2.0 * (z @ z.T)
        d2 = jnp.maximum(d2, 0.0)
        S = jnp.sqrt(d2 + 1e-10)
        S = jnp.exp(-S / (2.0 * sigma))
        order = jnp.argsort(-S, axis=-1)
        ranks = jnp.argsort(order, axis=-1)
        S = jnp.where(ranks < k, S, 0.0)
        A2 = S + A
        out = _lap_mul(A2, x) @ W2 + b2
        return out

    h = jnp.maximum(_layernorm(x, axis=-1), 0.0)
    x = x + _L0_gnn_ref(h, adj, L0_gnn_W1, L0_gnn_b1, L0_gnn_W2, L0_gnn_b2, 1, 4)
    return x


_drawn_inputs = setup_inputs


def setup_inputs(seed=0):
    import zlib

    import numpy as np

    out = dict(_drawn_inputs(seed))
    spreads = {}
    factors = {}
    for name, (base, spread) in spreads.items():
        noise = np.random.default_rng([zlib.crc32(name.encode()), seed]).standard_normal(out[name].shape)
        drawn = base * np.exp(spread * noise) if base else spread * noise
        out[name] = jnp.asarray(drawn.astype(out[name].dtype))
    for name, factor in factors.items():
        out[name] = (out[name] * factor).astype(out[name].dtype)
    return out
```

```python
from contextlib import ExitStack

import concourse.bass as bass
from concourse import mybir

F32 = mybir.dt.float32
F32R = mybir.dt.float32r
BF16 = mybir.dt.bfloat16
U32 = mybir.dt.uint32
ACT = mybir.ActivationFunctionType
ALU = mybir.AluOpType
AX_X = mybir.AxisListType.X

P = 128
LN_EPS = 1e-5
DIST_EPS = 1e-10
SLOPE = 0.1
TOP = 4
W = 512
JT = W // P
HB = 4
RING = 4
BLK = 8
LAG = 2


def gnn_kernel(nc, x, adj, W1, b1, W2, b2, out):
    N, D = x.shape
    T = N // P
    C = N // W
    QUADS = C // RING
    ITEMS = C * JT
    QI = RING * JT
    NB = T // BLK
    C_SIM = NB - LAG
    LNG = 8
    ZP = 2 * W
    NP = N // ZP
    HALF = W // 2

    ctx = ExitStack()
    with ctx:
        def sb(name, shape, dt=F32):
            return ctx.enter_context(nc.sbuf_tensor(name, shape, dt))

        def sem(name):
            return ctx.enter_context(nc.semaphore(name))

        acc = sb("acc", [P, N])
        zTH = sb("zTH", [P, N], F32R)
        zTL = sb("zTL", [P, N], F32R)
        itemH = sb("itemH", [P, HB, W], F32R)
        itemL = sb("itemL", [P, HB, W], F32R)
        hsH = sb("hsH", [P, JT, D], F32R)
        hsL = sb("hsL", [P, JT, D], F32R)
        z2H = sb("z2H", [P, 2, P], F32R)
        z2L = sb("z2L", [P, 2, P], F32R)
        ident = sb("ident", [P, P])
        negones = sb("negones", [P, P], BF16)
        rowsum = sb("rowsum", [P, T])
        dinv = sb("dinv", [P, T])
        sq = sb("sq", [P, T])
        S4 = sb("S4", [P, T, TOP])
        I4 = sb("I4", [P, T, TOP], U32)
        idx8 = sb("idx8", [P, 8], U32)
        top8 = sb("top8", [P, BLK, 8])
        dist = sb("dist", [P, BLK, TOP])
        hs_stage = sb("hs_stage", [P, JT, D])
        hrow = sb("hrow", [P, BLK // 2, D])
        ARENA = 20480
        arena = sb("arena", [P, ARENA])

        def view(at, *shape):
            n = 1
            for s in shape:
                n *= s
            assert at + n <= ARENA
            v = arena[:, at:at + n]
            if len(shape) == 2:
                v = v.rearrange("p (a b) -> p a b", b=shape[1])
            if len(shape) == 3:
                v = v.rearrange("p (a b c) -> p a b c", b=shape[1], c=shape[2])
            return v

        ring = view(0, RING, JT, W)
        RINGW = RING * JT * W
        h_all = view(RINGW, T, D)
        xg = view(RINGW + T * D, 2 * LNG, D)
        lt = view(RINGW + T * D + 2 * LNG * D, LNG, D)
        st = view(RINGW + T * D + 3 * LNG * D, 4, LNG)
        rs_part = view(RINGW + T * D + 3 * LNG * D + 4 * LNG, T, RING)
        w1s = view(0, D)
        b1bc = view(D, D)
        us = view(2 * D, 2, W)
        wt = view(2 * D + 2 * W, 2, W)
        zt = view(2 * D + 4 * W, 2, W)
        zjunk = view(2 * D + 6 * W, 2, W)
        sqr = view(2 * D + 8 * W, T)
        sqp = view(2 * D + 8 * W + T, 3 * T // 2).bitcast(BF16)
        sqt = view(2 * D + 8 * W + T + 3 * T // 2, 3 * P // 2).bitcast(BF16)
        identb = view(2 * D + 8 * W + 4 * T + 2 * P, P // 2).bitcast(BF16)
        v = view(0, 2, N)
        ringh = view(2 * N, 2 * JT, HALF)
        tcopy = view(2 * N + 2 * JT * HALF, 2, W)
        sqrow = view(2 * N + 2 * JT * HALF + 2 * W, N // 8).bitcast(BF16)
        nbr = view(RINGW, 2 * TOP, D)
        nbrs = view(RINGW + 2 * TOP * D, 2 * TOP, D)
        nsum = view(RINGW + 4 * TOP * D, 2, D)
        F6 = RINGW + 4 * TOP * D + 2 * D
        w2s = view(F6, D)
        b2bc = view(F6 + D, D)
        accs = view(F6 + 2 * D, 2, W)
        ot = view(F6 + 2 * D + 2 * W, 2 * JT, D)
        xb = view(0, T, D)
        idx = sb("idx", [P, 2, TOP], U32)
        rt = sb("rt", [P, 2, T])
        spare = sb("spare", [P, 4])

        tb = [ctx.enter_context(nc.psum_tensor(f"tb{i}", [P, W], F32)) for i in range(2)]
        ab = [ctx.enter_context(nc.psum_tensor(f"ab{i}", [P, W], F32)) for i in range(2)]
        zz = [ctx.enter_context(nc.psum_tensor(f"zz{i}", [P, ZP], F32)) for i in range(2)]
        tbank = [tb[0][:, :], tb[1][:, :], zz[0][:, 0:W], zz[0][:, W:ZP]]
        nbank = [zz[1][:, 0:P], zz[1][:, W:W + P]]

        h_dram = nc.dram_tensor("h_dram", (N, D), F32, kind="Internal").ap()
        hs_dram = nc.dram_tensor("hs_dram", (N, D), F32, kind="Internal").ap()
        sq_dram = nc.dram_tensor("sq_dram", (3, N), BF16, kind="Internal").ap()

        A_rows = adj.rearrange("(t p) (k w) -> t k p w", p=P, k=RING)
        A_groups = adj.rearrange("(g r p) (c w) -> g c p r w", r=JT, p=P, w=W)
        A_halves = adj.rearrange("(g r p) (c e w) -> g c e p r w", r=JT, p=P, e=2, w=HALF)
        x_ln = x.rearrange("(g t p) d -> g p t d", t=LNG, p=P)
        h_ln = h_dram.rearrange("(g t p) d -> g p t d", t=LNG, p=P)
        HBK = BLK // 2
        h_half = h_dram.rearrange("(g t p) d -> g p t d", t=HBK, p=P)
        hs_half = hs_dram.rearrange("(g t p) d -> g p t d", t=HBK, p=P)
        hs_chunk = hs_dram.rearrange("(c t p) d -> c p t d", t=JT, p=P)
        x_slot = x.rearrange("(k t p) d -> k p t d", t=T // RING, p=P)
        out_v = out.rearrange("(g t p) d -> g p t d", t=JT, p=P)

        consts = sem("consts")
        x_loaded = [sem(f"x_loaded{i}") for i in range(2)]
        h_made = sem("h_made")
        h_stored = sem("h_stored")
        part_loaded = [sem(f"part_loaded{i}") for i in range(RING)]
        part_summed = sem("part_summed")
        root_in = sem("root_in")
        root_out = sem("root_out")
        dve_step = sem("dve_step")
        act_step = sem("act_step")
        pool_step = sem("pool_step")
        hs_made = sem("hs_made")
        acc_zero = sem("acc_zero")
        a_loaded = [sem(f"a_loaded{i}") for i in range(RING)]
        t_ready = sem("t_ready")
        h_ready = sem("h_ready")
        l_ready = sem("l_ready")
        t_copied = sem("t_copied")
        m_done = sem("m_done")
        acc_added = sem("acc_added")
        hsh_ready = sem("hsh_ready")
        hsl_ready = sem("hsl_ready")
        stage_loaded = sem("stage_loaded")
        ah_loaded = [sem(f"ah_loaded{i}") for i in range(2)]

        w_loaded = sem("w_loaded")
        w2_loaded = sem("w2_loaded")
        u_ready = sem("u_ready")
        us_ready = sem("us_ready")
        ut_ready = sem("ut_ready")
        z_made = sem("z_made")
        z_used = sem("z_used")
        zt_ready = sem("zt_ready")
        zh_ready = sem("zh_ready")
        zl_ready = sem("zl_ready")
        sqp_made = sem("sqp_made")
        sqt_ready = sem("sqt_ready")
        sqt_copied = sem("sqt_copied")
        sq_stored = sem("sq_stored")
        sq_loaded = sem("sq_loaded")
        z2_ready = sem("z2_ready")
        zz_ready = sem("zz_ready")
        v_copied = sem("v_copied")
        top_found = sem("top_found")
        dist_made = sem("dist_made")
        s_made = sem("s_made")
        hrow_loaded = sem("hrow_loaded")
        hrow_made = sem("hrow_made")
        hs_stored = sem("hs_stored")
        nbr_loaded = [sem(f"nbr_loaded{i}") for i in range(2)]
        idx_ready = sem("idx_ready")
        nbr_scaled = sem("nbr_scaled")
        nsum_made = sem("nsum_made")
        nsum_turned = sem("nsum_turned")
        nsum_added = sem("nsum_added")
        accs_ready = sem("accs_ready")
        o_ready = sem("o_ready")
        o_made = sem("o_made")
        o_scaled = sem("o_scaled")
        x2_loaded = [sem(f"x2_loaded{i}") for i in range(RING)]
        xb_made = sem("xb_made")
        out_stored = [sem(f"out_stored{i}") for i in range(2)]

        TR = (RING - 1) * JT + 1
        ITEM2 = C * ITEMS
        RG2 = C * C
        ITEM5 = ITEM2 + C_SIM * ITEMS
        RG5 = RG2 + C_SIM * C

        ORDER = ("T0 T1 Z0 Z1 Z2 T2 M0 Z3 Z4 T3 M1 Z5 Z6 T4 M2 Z7 Z8 T5 M3 Z9 Z10 T6 M4 Z11 T7 M5 "
                 "Z12 Z13 M6 Z14 Z15 M7").split()
        ORDER = [(s[0], int(s[1:])) for s in ORDER]
        SIM_ONLY = [s for s in ORDER if s[0] == "Z"]

        block = ctx.enter_context(nc.Block())

        C_NBR = T // (2 * QUADS)

        @block.sync
        def _(sp):
            for e in range(2):
                sp.nop().then_inc(out_stored[e], 16)
            for k in range(RING):
                sp.dma_start(ring[:, k].rearrange("p a b -> p (a b)"), A_rows[0, k]).then_inc(part_loaded[k], 16)
            with sp.Fori(1, T) as t:
                for k in range(RING):
                    sp.wait_ge(part_summed, t * RING - RING + k + 1)
                    sp.dma_start(ring[:, k].rearrange("p a b -> p (a b)"), A_rows[t, k]).then_inc(part_loaded[k], 16)
            sp.wait_ge(part_summed, T * RING)

            def load_groups(c0, c1, rg0):
                with sp.Fori(c0, c1) as c:
                    with sp.Fori(0, QUADS) as q:
                        for k in range(RING):
                            sp.wait_ge(t_ready, (c - c0) * ITEMS + q * QI + (rg0 * JT + k * JT + 1))
                            sp.dma_start(ring[:, k], A_groups[q * RING + k, c]).then_inc(a_loaded[k], 16)

            load_groups(0, C, 0)

            with sp.Fori(0, C_SIM) as c:
                with sp.Fori(0, C) as g:
                    for e in range(2):
                        sp.wait_ge(t_ready, c * ITEMS + g * JT + (ITEM2 + TR + (JT // 2) * (e - 1)))
                        sp.dma_start(ringh[:, e * JT:e * JT + JT], A_halves[g, c, e]).then_inc(ah_loaded[e], 16)
            sp.wait_ge(top_found, T + 2)
            load_groups(C_SIM, C, RG5)
            for k in range(RING):
                sp.wait_ge(t_ready, 2 * ITEM2 + TR)
                sp.dma_start(xb[:, k * (T // RING):(k + 1) * (T // RING)], x_slot[k]).then_inc(x2_loaded[k], 16)
            with sp.Fori(0, C // 2) as gg:
                for e in range(2):
                    sp.wait_ge(o_made, gg * 2 + e + 3)
                    sp.dma_start(out_v[gg * 2 + e], ot[:, e * JT:(e + 1) * JT]).then_inc(out_stored[e], 16)
            for e in range(2):
                sp.wait_ge(out_stored[e], 16 * (C // 2) + 16)

        @block.scalar
        def _(act):
            act.nop().then_inc(us_ready, 2)
            act.nop().then_inc(z_used, 2 * JT)
            with act.Fori(0, T) as t:
                for k in range(RING):
                    piece = ring[:, k].rearrange("p a b -> p (a b)")
                    act.wait_ge(part_loaded[k], t * 16 + 16)
                    act.activation(piece, piece, ACT.Copy,
                                   accum_out=rs_part[:, bass.ds(t, 1), k]).then_inc(part_summed, 1)

            roots = [0]

            def root(dst, src):
                act.wait_ge(root_in, roots[0] + 1)
                act.activation(dst, src, ACT.Sqrt).then_inc(root_out, 1)
                roots[0] += 1

            for _g in range(T // LNG):
                root(st[:, 3], st[:, 2])
            root(dinv[:, :], rt[:, 0, :])

            act.wait_ge(hs_made, 1)

            def split_quad(item, first, hs_src):
                for k in range(QI):
                    act.wait_ge(t_ready, item + (k + 1 + TR))
                    act.wait_ge(m_done, item + k + 1)
                    act.activation(itemH[:, k % HB], tbank[k % 4], ACT.Copy).then_inc(h_ready, 1)
                    if first and k < JT:
                        act.activation(hsH[:, k], hs_src(k), ACT.Copy).then_inc(hsh_ready, 1)

            with act.Fori(0, C) as c:
                split_quad(c * ITEMS, True,
                           lambda k: h_all[:, bass.ds(c * JT + k, 1), :].rearrange("p a d -> p (a d)"))
                with act.Fori(1, QUADS) as q:
                    split_quad(c * ITEMS + q * QI, False, None)

            with act.Fori(0, C // 2) as gg:
                for e in range(2):
                    act.wait_ge(u_ready, gg * 2 + e + 1)
                    act.activation(us[:, e], tbank[2 + e], ACT.Copy).then_inc(us_ready, 1)
                act.wait_ge(z_used, gg * (2 * JT) + 2 * JT)
                for e in range(2):
                    g = gg * 2 + e
                    act.wait_ge(z_made, g + 3)
                    for r in range(JT):
                        act.activation(zjunk[:, e, r * P:(r + 1) * P], zt[:, e, r * P:(r + 1) * P], ACT.Square,
                                       accum_out=sq[:, bass.ds(g * JT + r, 1)]).then_inc(z_used, 1)
                    act.wait_ge(zt_ready, g + 1)
                    act.activation(zTH[:, bass.ds(g * W, W)], tb[e][:, :], ACT.Copy).then_inc(zh_ready, 1)

            act.nop().then_inc(t_copied, 2)

            def sim_tile(t, par, order, item):
                for what, k in order:
                    if what == "T":
                        act.wait_ge(t_ready, item + (k + 1 + TR))
                        act.wait_ge(l_ready, item + k)
                        act.activation(tcopy[:, k % 2], tb[k % 2][:, :], ACT.Copy).then_inc(t_copied, 1)
                        act.wait_ge(m_done, item + k + 1)
                        act.wait_ge(t_copied, item + (k + 3 - ITEM2))
                        act.activation(itemH[:, k % HB], tcopy[:, k % 2], ACT.Copy).then_inc(h_ready, 1)
                    if what == "Z" and k % 2:
                        pr = k // 2
                        if pr == 0:
                            act.wait_ge(top_found, t + 1)
                        act.wait_ge(zz_ready, t * NP + pr + 1)
                        act.activation(v[:, par, pr * ZP:(pr + 1) * ZP], zz[pr % 2][:, :],
                                       ACT.Copy).then_inc(v_copied, 1)

            def sim_pair(b, pair, order):
                for par in range(2):
                    t = b * BLK + (2 * pair + par)
                    sim_tile(t, par, order, (b - LAG) * ITEMS + (ITEM2 + (2 * pair + par) * 2 * JT))

            def similarities(b):
                act.wait_ge(dist_made, b + 1)
                act.activation(dist[:, :, :], dist[:, :, :], ACT.Sqrt).then_inc(act_step, 1)
                act.wait_ge(act_step, b + 1)
                act.activation(dist[:, :, :], dist[:, :, :], ACT.Exp, scale=-0.5).then_inc(s_made, 1)

            def block_root(b):
                act.wait_ge(root_in, b + (roots[0] + 1))
                act.activation(rt[:, 1, BLK:2 * BLK], rt[:, 0, 0:BLK], ACT.Sqrt).then_inc(root_out, 1)

            def sim_block(b, order, post):
                sim_pair(b, 0, order)
                if post:
                    similarities(b - 1)
                sim_pair(b, 1, order)
                if post:
                    block_root(b - 1)
                sim_pair(b, 2, order)
                sim_pair(b, 3, order)

            def stage_split(count, k):
                act.wait_ge(stage_loaded, count)
                act.activation(hsH[:, k], hs_stage[:, k], ACT.Copy).then_inc(hsh_ready, 1)

            sim_block(0, SIM_ONLY, False)
            sim_block(1, SIM_ONLY, True)
            with act.Fori(LAG, NB) as b:
                act.wait_ge(m_done, (b - LAG) * ITEMS + (ITEM2 + HB))
                for k in range(JT):
                    stage_split((b - LAG) * 16 + 16, k)
                sim_block(b, ORDER, True)
            similarities(NB - 1)
            block_root(NB - 1)

            with act.Fori(C_SIM, C) as c:
                act.wait_ge(stage_loaded, c * 16 + 16)
                split_quad((c - C_SIM) * ITEMS + ITEM5, True, lambda k: hs_stage[:, k])
                with act.Fori(1, QUADS) as q:
                    split_quad((c - C_SIM) * ITEMS + q * QI + ITEM5, False, None)

            act.wait_ge(acc_added, 2 * RG2 + 2)
            act.wait_ge(nsum_added, T + 2)
            act.wait_ge(m_done, 2 * ITEM2 + HB)
            with act.Fori(0, C // 2) as gg:
                for e in range(2):
                    g = gg * 2 + e
                    if e == 0:
                        act.wait_ge(o_ready, gg * 2 + 2)
                    act.activation(accs[:, e], acc[:, bass.ds(g * W, W)], ACT.Copy).then_inc(accs_ready, 1)

        @block.gpsimd
        def _(pool):
            steps = [0]

            def step(ins):
                steps[0] += 1
                ins.then_inc(pool_step, 1)
                pool.wait_ge(pool_step, steps[0])

            pool.dma_start(xg[:, 0:LNG], x_ln[0]).then_inc(x_loaded[0], 16)
            pool.dma_start(xg[:, LNG:2 * LNG], x_ln[1]).then_inc(x_loaded[1], 16)
            step(pool.memset(ident[:, :], 0.0))
            step(pool.affine_select(out=ident[:, :], in_=ident[:, :], compare_op=ALU.not_equal, fill=1.0,
                                    base=0, pattern=[[-1, P]], channel_multiplier=1))
            step(pool.memset(negones[:, :], -1.0))
            step(pool.memset(spare[:, 0:1], 0.0))
            pool.nop().then_inc(consts, 1)
            for g in range(T // LNG):
                pool.wait_ge(h_made, g + 1)
                pool.dma_start(h_ln[g], h_all[:, g * LNG:(g + 1) * LNG]).then_inc(h_stored, 16)
                if g + 2 < T // LNG:
                    e = g % 2
                    pool.dma_start(xg[:, e * LNG:(e + 1) * LNG], x_ln[g + 2]).then_inc(x_loaded[e], 16)
            pool.memset(acc[:, :], 0.0).then_inc(acc_zero, 1)

            pool.wait_ge(t_ready, ITEM2 + TR)
            pool.dma_start(w1s, W1).then_inc(w_loaded, 16)
            pool.dma_start(b1bc, b1.partition_broadcast(P)).then_inc(w_loaded, 16)
            pool.wait_ge(u_ready, C)
            pool.memset(acc[:, :], 0.0).then_inc(acc_zero, 1)
            pool.wait_ge(sqt_copied, 3)
            for k in range(3):
                pool.dma_start(sq_dram[k].rearrange("(t p) -> t p", p=P), sqt[0:T, k * P:(k + 1) * P]).then_inc(sq_stored, 16)
            pool.wait_ge(sq_stored, 48)
            pool.wait_ge(h_stored, 16 * (T // LNG))
            for q in range(4):
                pool.dma_start(sqrow[32 * q:32 * q + 3, :], sq_dram[:, q * (N // 4):(q + 1) * (N // 4)]).then_inc(sq_loaded, 16)
            pool.wait_ge(zl_ready, C + 2)
            pool.wait_ge(zh_ready, C)

            def low(item, k):
                pool.wait_ge(h_ready, item + k + 1)
                pool.tensor_tensor(itemL[:, k % HB], tcopy[:, k % 2], itemH[:, k % HB].bitcast(F32),
                                   ALU.subtract).then_inc(l_ready, 1)

            def sim_pair(b, pair, order):
                for par in range(2):
                    t = b * BLK + (2 * pair + par)
                    item = (b - LAG) * ITEMS + (ITEM2 + (2 * pair + par) * 2 * JT)
                    if not isinstance(t, int) or t >= 2:
                        pool.wait_ge(zz_ready, t * NP - NP)
                    for dst, src in ((z2H, zTH), (z2L, zTL)):
                        z = src[:, bass.ds(t * P, P)].bitcast(F32)
                        pool.tensor_tensor(dst[:, par], z, z, ALU.add).then_inc(z2_ready, 1)
                    for what, k in order:
                        if what == "T":
                            low(item, k)

            def load_hrow(half):
                pool.dma_start(hrow[:, :, :], h_half[half]).then_inc(hrow_loaded, 16)

            def store_hrow(half):
                pool.wait_ge(hrow_made, half + 1)
                pool.dma_start(hs_half[half], hrow[:, :, :]).then_inc(hs_stored, 16)

            def post_a(b):
                store_hrow(b * 2)
                pool.wait_ge(hs_stored, b * 32 + 16)
                load_hrow(b * 2 + 1)

            def load_stage(c):
                pool.wait_ge(hs_stored, c * 16 + 16)
                pool.wait_ge(hsh_ready, c * JT + C * JT)
                pool.wait_ge(hsl_ready, c * JT + C * JT)
                pool.dma_start(hs_stage[:, :, :], hs_chunk[c]).then_inc(stage_loaded, 16)

            def sim_block(b, order, post):
                if post:
                    load_hrow(b * 2 - 2)
                sim_pair(b, 0, order)
                sim_pair(b, 1, order)
                sim_pair(b, 2, order)
                if post:
                    post_a(b - 1)
                sim_pair(b, 3, order)
                if post:
                    store_hrow(b * 2 - 1)
                    pool.wait_ge(hs_stored, b * 32)
                    load_stage(b - 1)

            sim_block(0, SIM_ONLY, False)
            sim_block(1, SIM_ONLY, True)
            with pool.Fori(LAG, NB) as b:
                for k in range(JT):
                    pool.wait_ge(hsh_ready, (b - LAG) * JT + (C * JT + k + 1))
                    pool.tensor_tensor(hsL[:, k], hs_stage[:, k], hsH[:, k].bitcast(F32),
                                       ALU.subtract).then_inc(hsl_ready, 1)
                sim_block(b, ORDER, True)
            load_hrow(2 * NB - 2)
            post_a(NB - 1)
            store_hrow(2 * NB - 1)
            pool.wait_ge(hs_stored, 32 * NB)

            def fetch(t, e):
                pool.wait_ge(nbr_scaled, t + 1)
                pool.tensor_copy(idx[:, e], I4[:, bass.ds(t, 1), :].rearrange("p a k -> p (a k)")).then_inc(idx_ready, 1)
                pool.wait_ge(idx_ready, t + 1)
                pool.tensor_tensor(spare[:, 1:2], spare[:, 0:1], spare[:, 0:1], ALU.add).then_inc(pool_step, 1)
                for k in range(TOP):
                    pool.indirect_dma_start(
                        nbr[:, e * TOP + k], None, hs_dram,
                        bass.IndirectOffsetOnAxis(ap=idx[:, e, k:k + 1], axis=0)).then_inc(nbr_loaded[e], 16)

            def scale(t, qd, e):
                pool.wait_ge(nbr_loaded[e], qd * (16 * TOP) + 16 * TOP)
                pool.wait_ge(nsum_made, t + 1)
                pool.tensor_tensor(nbrs[:, e * TOP:(e + 1) * TOP], nbr[:, e * TOP:(e + 1) * TOP],
                                   S4[:, bass.ds(t, 1), :].rearrange("p a k -> p (a k)").unsqueeze(2)
                                   .to_broadcast([P, TOP, D]), ALU.mult).then_inc(nbr_scaled, 1)

            def quad_neighbours(qd, last=False):
                fetch(qd * 2 + 1, 1)
                scale(qd * 2, qd, 0)
                if not last:
                    fetch(qd * 2 + 2, 0)
                scale(qd * 2 + 1, qd, 1)

            pool.nop().then_inc(nbr_scaled, 2)
            fetch(0, 0)
            with pool.Fori(0, C_NBR - 1) as c:
                load_stage(c + (C_SIM + 1))
                with pool.Fori(0, QUADS) as q:
                    quad_neighbours(c * QUADS + q)
            load_stage(C_SIM + C_NBR)
            with pool.Fori((C_NBR - 1) * QUADS, C_NBR * QUADS - 1) as qd:
                quad_neighbours(qd)
            quad_neighbours(C_NBR * QUADS - 1, last=True)
            for c in range(C_SIM + C_NBR + 1, C):
                load_stage(c)

            pool.dma_start(w2s, W2).then_inc(w2_loaded, 16)
            pool.dma_start(b2bc, b2.partition_broadcast(P)).then_inc(w2_loaded, 16)
            pool.wait_ge(w2_loaded, 32)
            for k in range(RING):
                pool.wait_ge(x2_loaded[k], 16)
            with pool.Fori(0, C // 2) as gg:
                for e in range(2):
                    xg4 = xb[:, bass.ds(gg * (2 * JT) + e * JT, JT), :]
                    pool.tensor_tensor(xg4, xg4, b2bc.unsqueeze(1).to_broadcast([P, JT, D]),
                                       ALU.add).then_inc(xb_made, 1)

        @block.vector
        def _(dve):
            class Steps:
                base, n = 0, 0

            def step(ins):
                Steps.n += 1
                ins.then_inc(dve_step, 1)
                dve.wait_ge(dve_step, Steps.base + Steps.n)

            roots = [0]

            def rsqrt(dst, s, tmp, before):
                dve.reciprocal(tmp, s).then_inc(root_in, 1)
                dve.wait_ge(root_in, before + 1)
                dve.wait_ge(root_out, before + 1)
                newton(dst, s, tmp)

            def newton(dst, s, tmp):
                step(dve.tensor_tensor(tmp, dst, dst, ALU.mult))
                step(dve.tensor_tensor(tmp, tmp, s, ALU.mult))
                step(dve.tensor_scalar(tmp, tmp, -0.5, 1.5, ALU.mult, ALU.add))
                step(dve.tensor_tensor(dst, dst, tmp, ALU.mult))

            def per_row(ap, d):
                return ap.unsqueeze(2).to_broadcast([P, ap.shape[1], d])

            dve.nop().then_inc(acc_added, 2)
            dve.nop().then_inc(l_ready, 1)
            dve.nop().then_inc(z_made, 2)
            dve.nop().then_inc(zl_ready, 2)
            dve.nop().then_inc(o_made, 2)
            for g in range(T // LNG):
                e = g % 2
                xs = xg[:, e * LNG:(e + 1) * LNG]
                dve.wait_ge(x_loaded[e], 16 * (g // 2) + 16)
                step(dve.reduce_sum(st[:, 0], xs, AX_X))
                step(dve.tensor_scalar(st[:, 0], st[:, 0], 1.0 / D, None, ALU.mult))
                step(dve.tensor_tensor(lt, xs, per_row(st[:, 0], D), ALU.subtract))
                step(dve.tensor_tensor(xs, lt, lt, ALU.mult))
                step(dve.reduce_sum(st[:, 1], xs, AX_X))
                step(dve.tensor_scalar(st[:, 1], st[:, 1], 1.0 / D, LN_EPS, ALU.mult, ALU.add))
                rsqrt(st[:, 3], st[:, 1], st[:, 2], g)
                step(dve.tensor_tensor(lt, lt, per_row(st[:, 3], D), ALU.mult))
                dve.tensor_scalar(h_all[:, g * LNG:(g + 1) * LNG], lt, 0.0, None, ALU.max).then_inc(h_made, 1)
            dve.wait_ge(part_summed, T * RING)
            step(dve.reduce_sum(rowsum[:, :], rs_part, AX_X))
            rsqrt(dinv[:, :], rowsum[:, :], rt[:, 0, :], T // LNG)
            dve.wait_ge(h_stored, 16 * (T // LNG))
            dve.wait_ge(h_made, T // LNG)
            for g in range(T // LNG):
                hg = h_all[:, g * LNG:(g + 1) * LNG]
                step(dve.tensor_tensor(hg, hg, per_row(dinv[:, g * LNG:(g + 1) * LNG], D), ALU.mult))
            dve.nop().then_inc(hs_made, 1)

            def add_group(bank, col, rg, sums=None):
                if sums is not None:
                    dve.wait_ge(nsum_added, sums + 2)
                dve.wait_ge(m_done, rg * JT + (JT + HB))
                dve.wait_ge(acc_added, rg + 2)
                dst = acc[:, bass.ds(col, W)]
                dve.tensor_tensor(dst, dst, ab[bank][:, :], ALU.add).then_inc(acc_added, 1)

            def split_quad(rg, col, prev_col, hs_src, nbr_qd=None):
                for k in range(QI):
                    dve.wait_ge(h_ready, rg * JT + k + 1)
                    dve.tensor_tensor(itemL[:, k % HB], tbank[k % 4], itemH[:, k % HB].bitcast(F32),
                                      ALU.subtract).then_inc(l_ready, 1)
                    if hs_src is not None and k < JT:
                        dve.wait_ge(hsh_ready, hs_src[1] * JT + (k + 1))
                        dve.tensor_tensor(hsL[:, k], hs_src[0](k), hsH[:, k].bitcast(F32),
                                          ALU.subtract).then_inc(hsl_ready, 1)
                    if k % JT == 2:
                        r = k // JT
                        sums = None if nbr_qd is None else nbr_qd * 2 + int(k > 8)
                        if r:
                            add_group((r - 1) % 2, col + (r - 1) * W, rg + (r - 1), sums)
                        elif prev_col is not None:
                            add_group((RING - 1) % 2, prev_col, rg - 1, sums)
                    if nbr_qd is not None and k in (4, 10):
                        e = int(k == 10)
                        t = nbr_qd * 2 + e
                        dve.wait_ge(nbr_scaled, t + 3)
                        dve.reduce_sum(nsum[:, e], nbrs[:, e * TOP:(e + 1) * TOP].rearrange("p k d -> p d k"),
                                       AX_X).then_inc(nsum_made, 1)
                    if nbr_qd is not None and k in (8, 14):
                        e = int(k == 14)
                        t = nbr_qd * 2 + e
                        dve.wait_ge(nsum_turned, t + 1)
                        dve.wait_ge(acc_added, rg + (3 + 2 * e))
                        dve.wait_ge(nsum_added, t + 2)
                        dst = acc[:, bass.ds(t * P, P)]
                        dve.tensor_tensor(dst, dst, nbank[e], ALU.add).then_inc(nsum_added, 1)

            LASTCOL = (C - 1) * W
            dve.wait_ge(acc_zero, 1)

            def product(c0, c1, rg0, hs_at, hs0, nbr0):
                def chunk(c, first):
                    rg = (c - c0) * C + rg0
                    nq = None if nbr0 is None else (c - c0) * QUADS
                    split_quad(rg, 0, None if first else LASTCOL, (lambda k: hs_at(c, k), c - c0 + hs0), nq)
                    with dve.Fori(1, QUADS) as q:
                        split_quad(q * RING + rg, q * (RING * W), q * (RING * W) - W, None,
                                   None if nbr0 is None else q + nq)
                return chunk

            chunk = product(0, C, 0,
                            lambda c, k: h_all[:, bass.ds(c * JT + k, 1), :].rearrange("p a d -> p (a d)"), 0, None)
            chunk(0, True)
            with dve.Fori(1, C) as c:
                chunk(c, False)
            add_group((RING - 1) % 2, LASTCOL, RG2 - 1)

            dve.wait_ge(w_loaded, 32)
            Steps.base, Steps.n = Steps.base + Steps.n, 0
            before = Steps.base
            with dve.Fori(0, C // 2) as gg:
                Steps.base, Steps.n = gg * 4 + before, 0
                for e in range(2):
                    g = gg * 2 + e
                    w3 = wt[:, e].rearrange("p (r d) -> p r d", d=D)
                    dve.wait_ge(ut_ready, g + 1)
                    step(dve.tensor_tensor(w3, ab[e][:, :].rearrange("p (r d) -> p r d", d=D),
                                           per_row(dinv[:, bass.ds(g * JT, JT)], D), ALU.mult))
                    step(dve.tensor_tensor(w3, w3, b1bc.unsqueeze(1).to_broadcast([P, JT, D]), ALU.add))
                    dve.wait_ge(z_used, gg * (2 * JT) + 2 * JT)
                    dve.scalar_tensor_tensor(out=zt[:, e], in0=wt[:, e], scalar=SLOPE, in1=wt[:, e],
                                             op0=ALU.mult, op1=ALU.max).then_inc(z_made, 1)
                for e in range(2):
                    g = gg * 2 + e
                    dve.wait_ge(zh_ready, g + 1)
                    cols = bass.ds(g * W, W)
                    dve.tensor_tensor(zTL[:, cols], tb[e][:, :], zTH[:, cols].bitcast(F32),
                                      ALU.subtract).then_inc(zl_ready, 1)
            Steps.base, Steps.n = before + 4 * (C // 2), 0
            part = [sqp[:, k * T:(k + 1) * T] for k in range(3)]
            dve.wait_ge(z_used, T + 2 * JT)
            step(dve.tensor_copy(part[0], sq[:, :]))
            step(dve.tensor_tensor(sqr, sq[:, :], part[0], ALU.subtract))
            step(dve.tensor_copy(part[1], sqr))
            step(dve.tensor_tensor(sqr, sqr, part[1], ALU.subtract))
            step(dve.tensor_copy(part[2], sqr))
            dve.wait_ge(consts, 1)
            dve.tensor_copy(identb, ident[:, :]).then_inc(sqp_made, 1)
            for k in range(3):
                dve.wait_ge(sqt_ready, k + 1)
                dve.tensor_copy(sqt[0:T, k * P:(k + 1) * P],
                                [tb[0], tb[1], ab[0]][k][0:T, 0:P // 2].bitcast(BF16)).then_inc(sqt_copied, 1)

            dve.nop().then_inc(v_copied, 2)
            dve.nop().then_inc(top_found, 2)
            dve.wait_ge(acc_zero, 2)

            def sim_tile(b, j, product):
                t = b * BLK + j
                if product:
                    for r in range(2):
                        g = 2 * j + r
                        add_group(r, g * W, (b - LAG) * C + (RG2 + g))
                dve.wait_ge(v_copied, t * NP + (NP + 2))
                dve.memset(spare[:, 2:3], 0.0).then_inc(dve_step, 1)
                dve.max(top8[:, j], v[:, j % 2]).then_inc(dve_step, 1)
                Steps.n += 2
                dve.wait_ge(dve_step, Steps.base + Steps.n)
                dve.memset(spare[:, 2:3], 0.0).then_inc(dve_step, 1)
                Steps.n += 1
                dve.max_index(idx8[:, :], top8[:, j], v[:, j % 2]).then_inc(top_found, 1)
                dve.wait_ge(top_found, t + 3)
                step(dve.tensor_copy(I4[:, bass.ds(t, 1), :].rearrange("p a k -> p (a k)"), idx8[:, 0:TOP]))

            def distances(b):
                step(dve.tensor_tensor(dist[:, :, :], per_row(sq[:, bass.ds(b * BLK, BLK)], TOP),
                                       top8[:, :, 0:TOP], ALU.subtract))
                dve.tensor_scalar(dist[:, :, :], dist[:, :, :], 0.0, DIST_EPS,
                                  ALU.max, ALU.add).then_inc(dist_made, 1)

            def degrees(b):
                cols = bass.ds(b * BLK, BLK)
                dve.wait_ge(s_made, b + 1)
                step(dve.tensor_copy(S4[:, cols, :], dist[:, :, :]))
                step(dve.reduce_sum(rt[:, 1, 0:BLK], dist[:, :, :], AX_X))
                step(dve.tensor_tensor(rt[:, 1, 0:BLK], rt[:, 1, 0:BLK], rowsum[:, cols], ALU.add))
                dve.reciprocal(rt[:, 0, 0:BLK], rt[:, 1, 0:BLK]).then_inc(root_in, 1)

            def refine(b):
                dve.wait_ge(root_out, b + (T // LNG + 2))
                newton(rt[:, 1, BLK:2 * BLK], rt[:, 1, 0:BLK], rt[:, 0, 0:BLK])
                step(dve.tensor_copy(dinv[:, bass.ds(b * BLK, BLK)], rt[:, 1, BLK:2 * BLK]))

            def scale_hrow(b, half):
                dve.wait_ge(hrow_loaded, b * 32 + (half * 16 + 16))
                dve.tensor_tensor(hrow[:, :, :], hrow[:, :, :],
                                  per_row(dinv[:, bass.ds(b * BLK + half * HBK, HBK)], D),
                                  ALU.mult).then_inc(hrow_made, 1)

            def sim_block(b, product, post):
                for j in range(BLK):
                    if post and j == 2:
                        degrees(b - 1)
                    if post and j == 4:
                        refine(b - 1)
                        scale_hrow(b - 1, 0)
                    if post and j == 6:
                        scale_hrow(b - 1, 1)
                    sim_tile(b, j, product)
                distances(b)

            sim_block(0, False, False)
            sim_block(1, False, True)
            start = Steps.base + Steps.n
            PER = 4 * BLK + 1 + 3 + 5
            with dve.Fori(LAG, NB) as b:
                Steps.base, Steps.n = (b - LAG) * PER + start, 0
                sim_block(b, True, True)
                assert Steps.n == PER
            Steps.base, Steps.n = start + (NB - LAG) * PER, 0
            degrees(NB - 1)
            refine(NB - 1)
            scale_hrow(NB - 1, 0)
            scale_hrow(NB - 1, 1)

            dve.nop().then_inc(nsum_made, 2)
            dve.nop().then_inc(nsum_added, 2)
            chunk = product(C_SIM, C, RG5, lambda c, k: hs_stage[:, k], C + C_SIM, 0)
            chunk(C_SIM, True)
            with dve.Fori(C_SIM + 1, C_SIM + C_NBR) as c:
                chunk(c, False)
            chunk = product(C_SIM, C, RG5, lambda c, k: hs_stage[:, k], C + C_SIM, None)
            with dve.Fori(C_SIM + C_NBR, C) as c:
                chunk(c, False)
            add_group((RING - 1) % 2, LASTCOL, 2 * RG2 - 1)

            with dve.Fori(0, C // 2) as gg:
                for e in range(2):
                    g = gg * 2 + e
                    o3 = ot[:, e * JT:(e + 1) * JT]
                    dve.wait_ge(o_ready, g + 3)
                    dve.wait_ge(out_stored[e], gg * 16 + 16)
                    dve.tensor_tensor(o3, ab[e][:, :].rearrange("p (r d) -> p r d", d=D),
                                      per_row(dinv[:, bass.ds(g * JT, JT)], D), ALU.mult).then_inc(o_scaled, 1)
                    dve.wait_ge(o_scaled, g + 1)
                    dve.wait_ge(xb_made, g + 1)
                    dve.tensor_tensor(o3, o3, xb[:, bass.ds(g * JT, JT), :], ALU.add).then_inc(o_made, 1)

        @block.tensor
        def _(pe):
            pe.nop().then_inc(t_ready, TR)
            pe.nop().then_inc(o_ready, 2)
            pe.nop().then_inc(m_done, HB)
            pe.wait_ge(consts, 1)

            def turn(k, item, quads, free=True):
                slot, jt = (k // JT) % RING, k % JT
                if jt == 0:
                    pe.wait_ge(a_loaded[slot], quads * 16 + (16 * (k // QI) + 16))
                if free:
                    pe.wait_ge(l_ready, item + (k - 2))
                for r in range(JT):
                    last = pe.transpose(tbank[k % 4][:, r * P:(r + 1) * P],
                                        ring[:, slot, r, jt * P:(jt + 1) * P], ident[:, :])
                last.then_inc(t_ready, 1)

            def multiply(k, item, rg, hs_count):
                jt, bank = k % JT, (k // JT) % 2
                pe.wait_ge(l_ready, item + (k + 2))
                pe.wait_ge(h_ready, item + k + 1)
                if jt == 0:
                    pe.wait_ge(acc_added, rg + (k // JT + 1))
                if hs_count is not None:
                    pe.wait_ge(hsl_ready, hs_count + jt + 1)
                dst = ab[bank][:, :]
                H, L = itemH[:, k % HB], itemL[:, k % HB]
                pe.matmul(dst, hsH[:, jt], H, start=jt == 0, stop=False)
                pe.matmul(dst, hsH[:, jt], L, start=False, stop=False)
                pe.matmul(dst, hsL[:, jt], H, start=False, stop=jt == JT - 1).then_inc(m_done, 1)

            LEAD = 3

            def quad(item, rg, quads, hs_count, last=False, nbr=None):
                for k in range(QI):
                    if k + LEAD < QI or not last:
                        turn(k + LEAD, item, quads)
                    multiply(k, item, rg, hs_count if k < JT else None)
                    if nbr is not None and k in (6, 12):
                        e = int(k == 12)
                        pe.wait_ge(nsum_made, nbr * 2 + (e + 3))
                        pe.wait_ge(nsum_added, nbr * 2 + (e + 1))
                        pe.transpose(nbank[e], nsum[:, e], ident[:, :]).then_inc(nsum_turned, 1)

            def product(c0, c1, item0, rg0, quad0, hs0, nbrs_of):
                for k in range(LEAD):
                    turn(k, item0, quad0, free=False)

                def chunk(c, quads=QUADS, nbr=False):
                    i, r, qd = (c - c0) * ITEMS + item0, (c - c0) * C + rg0, (c - c0) * QUADS + quad0
                    hs = ((c - c0) + hs0) * JT
                    with pe.Fori(0, quads) as q:
                        quad(q * QI + i, q * RING + r, q + qd, hs, nbr=(c - c0) * QUADS + q if nbr else None)

                if nbrs_of:
                    with pe.Fori(c0, c0 + nbrs_of) as c:
                        chunk(c, nbr=True)
                with pe.Fori(c0 + nbrs_of, c1 - 1) as c:
                    chunk(c)
                chunk(c1 - 1, QUADS - 1)
                n = c1 - c0
                quad(item0 + n * ITEMS - QI, rg0 + n * C - RING, quad0 + n * QUADS - 1,
                     (n - 1 + hs0) * JT, last=True)

            product(0, C, 0, 0, 0, 0, 0)

            pe.wait_ge(acc_added, RG2 + 2)
            pe.wait_ge(w_loaded, 32)
            pe.wait_ge(l_ready, ITEM2 + 1)
            with pe.Fori(0, C // 2) as gg:
                for e in range(2):
                    g = gg * 2 + e
                    pe.wait_ge(us_ready, gg * 2 + 2)
                    pe.matmul(tbank[2 + e], w1s, acc[:, bass.ds(g * W, W)], start=True,
                              stop=True).then_inc(u_ready, 1)
                for e in range(2):
                    g = gg * 2 + e
                    pe.wait_ge(us_ready, g + 3)
                    pe.wait_ge(z_made, gg * 2 + 2)
                    for r in range(JT):
                        last = pe.transpose(ab[e][:, r * P:(r + 1) * P], us[:, e, r * P:(r + 1) * P], ident[:, :])
                    last.then_inc(ut_ready, 1)
                for e in range(2):
                    g = gg * 2 + e
                    pe.wait_ge(z_made, g + 3)
                    pe.wait_ge(zl_ready, gg * 2 + 2)
                    for r in range(JT):
                        last = pe.transpose(tb[e][:, r * P:(r + 1) * P], zt[:, e, r * P:(r + 1) * P], ident[:, :])
                    last.then_inc(zt_ready, 1)
            pe.wait_ge(sqp_made, 1)
            pe.wait_ge(zl_ready, C + 2)
            for k in range(3):
                pe.transpose([tb[0], tb[1], ab[0]][k][0:T, 0:P // 2].bitcast(BF16), sqp[:, k * T:(k + 1) * T],
                             identb).then_inc(sqt_ready, 1)

            pe.wait_ge(sqt_copied, 3)
            pe.wait_ge(sq_loaded, 64)
            pe.wait_ge(zh_ready, C)

            def sim_tile(b, j, par, order):
                t = b * BLK + j
                if len(order) > len(SIM_ONLY):
                    item, rg = (b - LAG) * ITEMS + (j * (2 * JT) + ITEM2), (b - LAG) * C + (j * 2 + RG2)
                pe.wait_ge(z2_ready, t * 2 + 2)
                for what, k in order:
                    if what == "T":
                        half, jt = (k // 2) % 2, k % 2
                        if jt == 0:
                            pe.wait_ge(ah_loaded[half], (b - LAG) * (16 * C) + (j * 32 + (16 * (k // JT) + 16)))
                        pe.wait_ge(t_copied, item + (k + 1 - ITEM2))
                        for r in range(JT):
                            last = pe.transpose(tb[k % 2][:, r * P:(r + 1) * P],
                                                ringh[:, half * JT + r, jt * P:(jt + 1) * P], ident[:, :])
                        last.then_inc(t_ready, 1)
                    if what == "M":
                        multiply(k, item, rg, (b - LAG + C) * JT)
                    if what == "Z":
                        pr, q = k // 2, k // 4
                        if k % 2 == 0:
                            pe.wait_ge(v_copied, t * NP + pr + 1)
                        dst = zz[pr % 2][:, (k % 2) * W:(k % 2 + 1) * W]
                        cols = slice(k * W, (k + 1) * W)
                        pe.matmul(dst, z2H[:, par], zTH[:, cols], start=True, stop=False)
                        pe.matmul(dst, z2H[:, par], zTL[:, cols], start=False, stop=False)
                        pe.matmul(dst, z2L[:, par], zTH[:, cols], start=False, stop=False)
                        last = pe.matmul(dst, negones[32 * q:32 * q + 3, :],
                                         sqrow[32 * q:32 * q + 3, (k % 4) * W:(k % 4 + 1) * W],
                                         start=False, stop=True)
                        if k % 2:
                            last.then_inc(zz_ready, 1)

            for b in range(LAG):
                with pe.Fori(0, BLK // 2) as pair:
                    for par in range(2):
                        sim_tile(b, pair * 2 + par, par, SIM_ONLY)
            with pe.Fori(LAG, NB) as b:
                with pe.Fori(0, BLK // 2) as pair:
                    for par in range(2):
                        sim_tile(b, pair * 2 + par, par, ORDER)

            pe.wait_ge(v_copied, T * NP + 2)
            pe.wait_ge(t_copied, C_SIM * ITEMS + 2)
            pe.wait_ge(l_ready, ITEM5 + 1)
            product(C_SIM, C, ITEM5, RG5, C * QUADS, C + C_SIM, C_NBR)

            pe.wait_ge(acc_added, 2 * RG2 + 2)
            pe.wait_ge(w2_loaded, 32)
            with pe.Fori(0, C // 2) as gg:
                for e in range(2):
                    g = gg * 2 + e
                    pe.wait_ge(accs_ready, g + 1)
                    pe.wait_ge(o_made, gg * 2 + 2)
                    for r in range(JT):
                        last = pe.matmul(ab[e][:, r * P:(r + 1) * P], accs[:, e, r * P:(r + 1) * P], w2s,
                                         start=True, stop=True)
                    last.then_inc(o_ready, 1)


_INS = ["x", "adj", "L0_gnn_W1", "L0_gnn_b1", "L0_gnn_W2", "L0_gnn_b2"]


def kernel(**inputs):
    import numpy as np
    import concourse.bacc as bacc
    from concourse.bass_utils import run_bass_kernel_spmd

    nc = bacc.Bacc("TRN2", target_bir_lowering=False, num_devices=1)
    arrays, args = {}, []
    for name in _INS:
        a = np.ascontiguousarray(inputs[name])
        arrays[name + "_in"] = a
        args.append(nc.dram_tensor(name + "_in", a.shape, mybir.dt.from_np(a.dtype), kind="ExternalInput").ap())
    out = nc.dram_tensor("out", inputs["x"].shape, F32, kind="ExternalOutput").ap()
    gnn_kernel(nc, *args, out)
    r = run_bass_kernel_spmd(nc, [arrays], core_ids=[0])
    return r.results[0]["out"]
```

```python
from contextlib import ExitStack

import concourse.bass as bass
from concourse import mybir

F32 = mybir.dt.float32
F32R = mybir.dt.float32r
BF16 = mybir.dt.bfloat16
U32 = mybir.dt.uint32
ACT = mybir.ActivationFunctionType
ALU = mybir.AluOpType
AX_X = mybir.AxisListType.X

P = 128
LN_EPS = 1e-5
DIST_EPS = 1e-10
SLOPE = 0.1

TOP = 4
W = 512
JT = W // P
HB = 4
RING = 4
BLK = 8
LAG = 2


def gnn_kernel(nc, x, adj, W1, b1, W2, b2, out):
    N, D = x.shape
    T = N // P
    C = N // W
    QUADS = C // RING
    ITEMS = C * JT
    QI = RING * JT
    SUP = C // RING
    ST = T // SUP
    BODIES = RING * RING
    ITEMS1 = [sum(BODIES * r * JT for r in range(s)) for s in range(SUP + 1)]
    QUADS2 = [sum(RING * (r + 1) for r in range(s)) for s in range(SUP + 1)]
    NB = T // BLK
    C_SIM = NB - LAG
    LNG = 8
    ZP = 2 * W
    NP = N // ZP
    HALF = W // 2

    ctx = ExitStack()
    with ctx:
        def sb(name, shape, dt=F32):
            return ctx.enter_context(nc.sbuf_tensor(name, shape, dt))

        def sem(name):
            return ctx.enter_context(nc.semaphore(name))

        acc = sb("acc", [P, N])
        zTH = sb("zTH", [P, N], F32R)
        zTL = sb("zTL", [P, N], F32R)
        itemH = sb("itemH", [P, HB, W], F32R)
        itemL = sb("itemL", [P, HB, W], F32R)
        hsH = sb("hsH", [P, JT, D], F32R)
        hsL = sb("hsL", [P, JT, D], F32R)
        z2H = sb("z2H", [P, 2, P], F32R)
        z2L = sb("z2L", [P, 2, P], F32R)
        ident = sb("ident", [P, P])
        negones = sb("negones", [P, P], BF16)
        rowsum = sb("rowsum", [P, T])
        dinv = sb("dinv", [P, T])
        sq = sb("sq", [P, T])
        S4 = sb("S4", [P, T, TOP])
        I4 = sb("I4", [P, T, TOP], U32)
        idx8 = sb("idx8", [P, 8], U32)
        top8 = sb("top8", [P, BLK, 8])
        dist = sb("dist", [P, BLK, TOP])
        hs_stage = sb("hs_stage", [P, JT, D])
        hrow = sb("hrow", [P, BLK // 2, D])
        ARENA = 20480
        HBK = BLK // 2
        arena = sb("arena", [P, ARENA])

        def view(at, *shape):
            n = 1
            for s in shape:
                n *= s
            assert at + n <= ARENA
            v = arena[:, at:at + n]
            if len(shape) == 2:
                v = v.rearrange("p (a b) -> p a b", b=shape[1])
            if len(shape) == 3:
                v = v.rearrange("p (a b c) -> p a b c", b=shape[1], c=shape[2])
            return v

        ring = view(0, RING, JT, W)
        RINGW = RING * JT * W
        h_all = view(RINGW, T, D)
        lt = view(RINGW + T * D, LNG, D)
        st = view(RINGW + T * D + LNG * D, 4, T)
        rs_part = view(RINGW + T * D + LNG * D + 4 * T, T, C)
        w1s = view(0, D)
        b1bc = view(D, D)
        us = view(2 * D, 2, W)
        wt = view(2 * D + 2 * W, 2, W)
        zt = view(2 * D + 4 * W, 2, W)
        zjunk = view(2 * D + 6 * W, 2, W)
        sqr = view(2 * D + 8 * W, T)
        sqp = view(2 * D + 8 * W + T, 3 * T // 2).bitcast(BF16)
        sqt = view(2 * D + 8 * W + T + 3 * T // 2, 3 * P // 2).bitcast(BF16)
        identb = view(2 * D + 8 * W + 4 * T + 2 * P, P // 2).bitcast(BF16)
        v = view(0, 2, N)
        ringh = view(2 * N, 2 * JT, HALF)
        tcopy = view(2 * N + 2 * JT * HALF, 2, W)
        sqrow = view(2 * N + 2 * JT * HALF + 2 * W, N // 8).bitcast(BF16)
        nbr = view(RINGW, 2 * TOP, D)
        nbrs = view(RINGW + 2 * TOP * D, 2 * TOP, D)
        nsum = view(RINGW + 4 * TOP * D, 2, D)
        hlast = view(RINGW + 4 * TOP * D + 2 * D, BLK, D)
        F6 = RINGW + 4 * TOP * D + 2 * D
        w2s = view(F6, D)
        b2bc = view(F6 + D, D)
        accs = view(F6 + 2 * D, 2, W)
        ot = view(F6 + 2 * D + 2 * W, 2 * JT, D)
        xb = view(0, T, D)
        idx = sb("idx", [P, 2, TOP], U32)
        rt = sb("rt", [P, 2, T])
        spare = sb("spare", [P, 2 + BLK])

        tb = [ctx.enter_context(nc.psum_tensor(f"tb{i}", [P, W], F32)) for i in range(2)]
        ab = [ctx.enter_context(nc.psum_tensor(f"ab{i}", [P, W], F32)) for i in range(2)]
        zz = [ctx.enter_context(nc.psum_tensor(f"zz{i}", [P, ZP], F32)) for i in range(2)]
        tbank = [tb[0][:, :], tb[1][:, :], zz[0][:, 0:W], zz[0][:, W:ZP]]
        nbank = [zz[1][:, 0:P], zz[1][:, W:W + P]]

        h_dram = nc.dram_tensor("h_dram", (N, D), F32, kind="Internal").ap()
        hs_dram = nc.dram_tensor("hs_dram", (N, D), F32, kind="Internal").ap()
        sq_dram = nc.dram_tensor("sq_dram", (3, N), BF16, kind="Internal").ap()

        A_groups = adj.rearrange("(g r p) (c w) -> g c p r w", r=JT, p=P, w=W)
        A_halves = adj.rearrange("(g r p) (c e w) -> g c e p r w", r=JT, p=P, e=2, w=HALF)
        x_ln = x.rearrange("(g t p) d -> g p t d", t=LNG, p=P)
        h_ln = h_dram.rearrange("(g t p) d -> g p t d", t=LNG, p=P)
        h_half = h_dram.rearrange("(g t p) d -> g p t d", t=HBK, p=P)
        hs_half = hs_dram.rearrange("(g t p) d -> g p t d", t=HBK, p=P)
        hs_chunk = hs_dram.rearrange("(c t p) d -> c p t d", t=JT, p=P)
        x_slot = x.rearrange("(k t p) d -> k p t d", t=T // RING, p=P)
        out_v = out.rearrange("(g t p) d -> g p t d", t=JT, p=P)

        consts = sem("consts")
        x_loaded = [sem(f"x_loaded{i}") for i in range(T // LNG)]
        h_made = sem("h_made")
        h_stored = sem("h_stored")
        summed = [sem(f"summed{i}") for i in range(RING)]
        root_in = sem("root_in")
        root_out = sem("root_out")
        dve_step = sem("dve_step")
        act_step = sem("act_step")
        pool_step = sem("pool_step")
        hs_made = sem("hs_made")
        a_loaded = [sem(f"a_loaded{i}") for i in range(RING)]
        t_ready = sem("t_ready")
        h_ready = sem("h_ready")
        l_ready = sem("l_ready")
        t_copied = sem("t_copied")
        m_done = sem("m_done")
        acc_added = sem("acc_added")
        hsh_ready = sem("hsh_ready")
        hsl_ready = sem("hsl_ready")
        stage_loaded = sem("stage_loaded")
        ah_loaded = [sem(f"ah_loaded{i}") for i in range(2)]

        w_loaded = sem("w_loaded")
        w2_loaded = sem("w2_loaded")
        u_ready = sem("u_ready")
        us_ready = sem("us_ready")
        ut_ready = sem("ut_ready")
        z_made = sem("z_made")
        z_used = sem("z_used")
        zt_ready = sem("zt_ready")
        zh_ready = sem("zh_ready")
        zl_ready = sem("zl_ready")
        sqp_made = sem("sqp_made")
        sqt_ready = sem("sqt_ready")
        sqt_copied = sem("sqt_copied")
        sq_stored = sem("sq_stored")
        sq_loaded = sem("sq_loaded")
        z2_ready = sem("z2_ready")
        zz_ready = sem("zz_ready")
        v_copied = sem("v_copied")
        top_found = sem("top_found")
        dist_made = sem("dist_made")
        s_made = sem("s_made")
        hrow_loaded = sem("hrow_loaded")
        hrow_made = sem("hrow_made")
        hs_stored = sem("hs_stored")
        nbr_loaded = [sem(f"nbr_loaded{i}") for i in range(2)]
        idx_ready = sem("idx_ready")
        nbr_scaled = sem("nbr_scaled")
        nsum_made = sem("nsum_made")
        nsum_turned = sem("nsum_turned")
        nsum_added = sem("nsum_added")
        accs_ready = sem("accs_ready")
        o_ready = sem("o_ready")
        o_made = sem("o_made")
        o_scaled = sem("o_scaled")
        x2_loaded = [sem(f"x2_loaded{i}") for i in range(RING)]
        xb_made = sem("xb_made")
        out_stored = [sem(f"out_stored{i}") for i in range(2)]

        TR = (RING - 1) * JT + 1
        ITEM2 = C * ITEMS
        RG1 = (SUP - 1) * RING
        RG2 = RG1 + QUADS2[SUP] * RING
        QUAD5 = SUP * BODIES + QUADS2[SUP]
        HS2 = ITEMS1[SUP] + C * JT
        ROOTS = 1 + SUP

        def act_sums(s):
            return range(RING) if s == 0 else (RING - 1,)

        def sums_first(s):
            return s < SUP - 1
        ITEM5 = ITEM2 + C_SIM * ITEMS
        RG5 = RG2 + C_SIM * C

        ORDER = ("T0 T1 Z0 Z1 Z2 T2 M0 Z3 Z4 T3 M1 Z5 Z6 T4 M2 Z7 Z8 T5 M3 Z9 Z10 T6 M4 Z11 T7 M5 "
                 "Z12 Z13 M6 Z14 Z15 M7").split()
        LAST_ORDER = ("T0 T1 Z0 Z1 Z2 Z3 Z4 Z5 Z6 Z7 Z8 Z9 Z10 Z11 Z12 Z13 Z14 Z15 T2 M0 T3 M1 T4 M2 "
                      "T5 M3 T6 M4 T7 M5 M6 M7").split()
        ORDER, LAST_ORDER = [[(s[0], int(s[1:])) for s in order] for order in (ORDER, LAST_ORDER)]
        SIM_ONLY = [s for s in ORDER if s[0] == "Z"]

        block = ctx.enter_context(nc.Block())

        C_NBR = T // (2 * QUADS)

        @block.sync
        def _(sp):
            for e in range(2):
                sp.nop().then_inc(out_stored[e], 16)
            for s in range(SUP):
                if s > 1:
                    sp.wait_ge(t_ready, ITEMS1[s] + TR)
                with sp.Fori(0, RING) as R:
                    with sp.Fori(0, RING) as q:
                        for k in range(RING):
                            if k < s:
                                sp.wait_ge(t_ready, R * (RING * s * JT) + q * (s * JT)
                                           + (ITEMS1[s] + TR - (s - 1 - k) * JT))
                            sp.wait_ge(summed[k], R * RING + q + (s * BODIES + 1))
                            sp.dma_start(ring[:, k], A_groups[R + s * RING, q + k * RING]).then_inc(a_loaded[k], 16)
            sp.wait_ge(t_ready, ITEMS1[SUP] + TR)
            for k in range(RING):
                sp.wait_ge(summed[k], SUP * BODIES + 1)

            def load_groups(c0, c1, quads, item0):
                with sp.Fori(c0, c1) as c:
                    with sp.Fori(0, quads) as q:
                        for k in range(RING):
                            sp.wait_ge(t_ready, (c - c0) * (quads * QI) + q * QI + (item0 + k * JT + 1))
                            sp.dma_start(ring[:, k], A_groups[q * RING + k, c]).then_inc(a_loaded[k], 16)

            for s in range(SUP):
                load_groups(s * RING, (s + 1) * RING, s + 1, ITEMS1[SUP] + QUADS2[s] * QI)

            with sp.Fori(0, C_SIM) as c:
                with sp.Fori(0, C) as g:
                    for e in range(2):
                        sp.wait_ge(t_ready, c * ITEMS + g * JT + (ITEM2 + TR + (JT // 2) * (e - 1)))
                        sp.dma_start(ringh[:, e * JT:e * JT + JT], A_halves[g, c, e]).then_inc(ah_loaded[e], 16)
            sp.wait_ge(top_found, T + 1)
            load_groups(C_SIM, C, QUADS, ITEM5)
            for k in range(RING):
                sp.wait_ge(t_ready, 2 * ITEM2 + TR)
                sp.dma_start(xb[:, k * (T // RING):(k + 1) * (T // RING)], x_slot[k]).then_inc(x2_loaded[k], 16)
            with sp.Fori(0, C // 2) as gg:
                for e in range(2):
                    sp.wait_ge(o_made, gg * 2 + e + 3)
                    sp.dma_start(out_v[gg * 2 + e], ot[:, e * JT:(e + 1) * JT]).then_inc(out_stored[e], 16)
            for e in range(2):
                sp.wait_ge(out_stored[e], 16 * (C // 2) + 16)

        @block.scalar
        def _(act):
            act.nop().then_inc(us_ready, 2)
            act.nop().then_inc(z_used, 2 * JT)
            roots = [0]

            def root(dst, src):
                act.wait_ge(root_in, roots[0] + 1)
                act.activation(dst, src, ACT.Sqrt).then_inc(root_out, 1)
                roots[0] += 1

            def hs_tile(tile):
                return h_all[:, bass.ds(tile, 1), :].rearrange("p a d -> p (a d)")

            def sum_rows(k, s, R, q):
                act.wait_ge(a_loaded[k], (R * RING + q) * 16 + (s * BODIES * 16 + 16))
                for r in range(JT):
                    part = rs_part[:, bass.ds((R + s * RING) * JT + r, 1), bass.ds(q + k * RING, 1)]
                    last = act.activation(ring[:, k, r], ring[:, k, r], ACT.Copy,
                                          accum_out=part.rearrange("p a b -> p (a b)"))
                last.then_inc(summed[k], 1)

            def first_rows(s, R, q):
                item = (R * RING + q) * (s * JT) + ITEMS1[s]
                for k in range(RING):
                    if k < s:
                        for jt in range(JT):
                            m = k * JT + jt
                            act.wait_ge(t_ready, item + (m + 1 + TR))
                            act.wait_ge(m_done, item + (m + 1))
                            act.activation(itemH[:, jt], tbank[jt], ACT.Copy).then_inc(h_ready, 1)
                            act.activation(hsH[:, jt], hs_tile((q + k * RING) * JT + jt),
                                           ACT.Copy).then_inc(hsh_ready, 1)
                    if k in act_sums(s):
                        sum_rows(k, s, R, q)

            for s in range(SUP):
                if s:
                    act.wait_ge(hs_made, s)
                if s == 0:
                    with act.Fori(0, RING) as q:
                        first_rows(0, 0, q)
                    root(st[:, 3], st[:, 2])
                with act.Fori(1 if s == 0 else 0, RING) as R:
                    with act.Fori(0, RING) as q:
                        first_rows(s, R, q)
                root(dinv[:, s * ST:(s + 1) * ST], rt[:, 0, s * ST:(s + 1) * ST])
            act.wait_ge(hs_made, SUP)

            def split_quad(item, first, hs_src, beside={}):
                for k in range(QI):
                    act.wait_ge(t_ready, item + (k + 1 + TR))
                    act.wait_ge(m_done, item + k + 1)
                    act.activation(itemH[:, k % HB], tbank[k % 4], ACT.Copy).then_inc(h_ready, 1)
                    if first and k < JT:
                        act.activation(hsH[:, k], hs_src(k), ACT.Copy).then_inc(hsh_ready, 1)
                    if k in beside:
                        beside[k]()

            for s in range(SUP):
                with act.Fori(s * RING, (s + 1) * RING) as c:
                    item = (c - s * RING) * ((s + 1) * QI) + (ITEMS1[SUP] + QUADS2[s] * QI)
                    split_quad(item, True, lambda k: hs_tile(c * JT + k))
                    if s:
                        with act.Fori(1, s + 1) as q:
                            split_quad(item + q * QI, False, None)

            with act.Fori(0, C // 2) as gg:
                for e in range(2):
                    act.wait_ge(u_ready, gg * 2 + e + 1)
                    act.activation(us[:, e], tbank[2 + e], ACT.Copy).then_inc(us_ready, 1)
                act.wait_ge(z_used, gg * (2 * JT) + 2 * JT)
                for e in range(2):
                    g = gg * 2 + e
                    act.wait_ge(z_made, g + 3)
                    for r in range(JT):
                        act.activation(zjunk[:, e, r * P:(r + 1) * P], zt[:, e, r * P:(r + 1) * P], ACT.Square,
                                       accum_out=sq[:, bass.ds(g * JT + r, 1)]).then_inc(z_used, 1)
                    act.wait_ge(zt_ready, g + 1)
                    act.activation(zTH[:, bass.ds(g * W, W)], tb[e][:, :], ACT.Copy).then_inc(zh_ready, 1)

            act.nop().then_inc(t_copied, 2)

            def sim_tile(t, par, order, item, hs_count=None):
                for what, k in order:
                    if what == "T":
                        act.wait_ge(t_ready, item + (k + 1 + TR))
                        act.wait_ge(l_ready, item + k)
                        act.activation(tcopy[:, k % 2], tb[k % 2][:, :], ACT.Copy).then_inc(t_copied, 1)
                        act.wait_ge(m_done, item + k + 1)
                        act.wait_ge(t_copied, item + (k + 3 - ITEM2))
                        act.activation(itemH[:, k % HB], tcopy[:, k % 2], ACT.Copy).then_inc(h_ready, 1)
                        if hs_count is not None and k < JT:
                            act.wait_ge(stage_loaded, hs_count)
                            act.activation(hsH[:, k], hs_stage[:, k], ACT.Copy).then_inc(hsh_ready, 1)
                    if what == "Z" and k % 2:
                        pr = k // 2
                        if pr == 0:
                            act.wait_ge(top_found, t + 1)
                        act.wait_ge(zz_ready, t * NP + pr + 1)
                        act.activation(v[:, par, pr * ZP:(pr + 1) * ZP], zz[pr % 2][:, :],
                                       ACT.Copy).then_inc(v_copied, 1)

            def sim_pair(b, pair, order, last=False):
                for par in range(2):
                    t = b * BLK + (2 * pair + par)
                    sim_tile(t, par, LAST_ORDER if last and par else order,
                             (b - LAG) * ITEMS + (ITEM2 + (2 * pair + par) * 2 * JT),
                             (b - LAG) * 16 + 16 if pair == 0 and par == 0 else None)

            def similarities(b):
                act.wait_ge(dist_made, b + 1)
                act.activation(dist[:, :, :], dist[:, :, :], ACT.Sqrt).then_inc(act_step, 1)
                act.wait_ge(act_step, b + 1)
                act.activation(dist[:, :, :], dist[:, :, :], ACT.Exp, scale=-0.5).then_inc(s_made, 1)

            def block_root(b):
                act.wait_ge(root_in, b + (roots[0] + 1))
                act.activation(rt[:, 1, BLK:2 * BLK], rt[:, 0, 0:BLK], ACT.Sqrt).then_inc(root_out, 1)

            def sim_block(b, order, post, last=False):
                sim_pair(b, 0, order)
                if post:
                    similarities(b - 1)
                sim_pair(b, 1, order)
                if post:
                    block_root(b - 1)
                sim_pair(b, 2, order)
                sim_pair(b, 3, order, last)



            sim_block(0, SIM_ONLY, False)
            sim_block(1, SIM_ONLY, True)
            with act.Fori(LAG, NB - 1) as b:
                sim_block(b, ORDER, True)
            sim_block(NB - 1, ORDER, True, last=True)

            act.wait_ge(stage_loaded, C_SIM * 16 + 16)
            split_quad(ITEM5, True, lambda k: hs_stage[:, k], {JT - 1: lambda: similarities(NB - 1)})
            split_quad(ITEM5 + QI, False, None, {QI // 2: lambda: block_root(NB - 1)})
            for q in range(2, QUADS):
                split_quad(ITEM5 + q * QI, False, None)
            with act.Fori(C_SIM + 1, C) as c:
                act.wait_ge(stage_loaded, c * 16 + 16)
                split_quad((c - C_SIM) * ITEMS + ITEM5, True, lambda k: hs_stage[:, k])
                with act.Fori(1, QUADS) as q:
                    split_quad((c - C_SIM) * ITEMS + q * QI + ITEM5, False, None)

            act.wait_ge(acc_added, RG2 + C * C + 2)
            act.wait_ge(nsum_added, T + 2)
            act.wait_ge(m_done, 2 * ITEM2 + HB)
            with act.Fori(0, C // 2) as gg:
                for e in range(2):
                    g = gg * 2 + e
                    if e == 0:
                        act.wait_ge(o_ready, gg * 2 + 2)
                    act.activation(accs[:, e], acc[:, bass.ds(g * W, W)], ACT.Copy).then_inc(accs_ready, 1)

        @block.gpsimd
        def _(pool):
            steps = [0]

            def step(ins):
                steps[0] += 1
                ins.then_inc(pool_step, 1)
                pool.wait_ge(pool_step, steps[0])

            for g in range(T // LNG):
                pool.dma_start(h_all[:, g * LNG:(g + 1) * LNG], x_ln[g]).then_inc(x_loaded[g], 16)
            step(pool.memset(ident[:, :], 0.0))
            step(pool.affine_select(out=ident[:, :], in_=ident[:, :], compare_op=ALU.not_equal, fill=1.0,
                                    base=0, pattern=[[-1, P]], channel_multiplier=1))
            step(pool.memset(negones[:, :], -1.0))
            step(pool.memset(spare[:, 0:1], 0.0))
            pool.nop().then_inc(consts, 1)
            for g in range(T // LNG):
                pool.wait_ge(h_made, g + 1)
                pool.dma_start(h_ln[g], h_all[:, g * LNG:(g + 1) * LNG]).then_inc(h_stored, 16)
            for s in range(1, SUP):
                pool.wait_ge(hs_made, s)
                with pool.Fori(0, RING) as R:
                    with pool.Fori(0, RING) as q:
                        for m in range(s * JT):
                            k, jt = m // JT, m % JT
                            tile = h_all[:, bass.ds(q * JT + (k * RING * JT + jt), 1), :]
                            pool.wait_ge(hsh_ready, R * (RING * s * JT) + q * (s * JT) + (ITEMS1[s] + m + 1))
                            pool.tensor_tensor(hsL[:, jt], tile.rearrange("p a d -> p (a d)"),
                                               hsH[:, jt].bitcast(F32), ALU.subtract).then_inc(hsl_ready, 1)

            pool.wait_ge(t_ready, ITEM2 + TR)
            pool.dma_start(w1s, W1).then_inc(w_loaded, 16)
            pool.dma_start(b1bc, b1.partition_broadcast(P)).then_inc(w_loaded, 16)
            pool.wait_ge(sqt_copied, 3)
            for k in range(3):
                pool.dma_start(sq_dram[k].rearrange("(t p) -> t p", p=P), sqt[0:T, k * P:(k + 1) * P]).then_inc(sq_stored, 16)
            pool.wait_ge(sq_stored, 48)
            pool.wait_ge(h_stored, 16 * (T // LNG))
            for q in range(4):
                pool.dma_start(sqrow[32 * q:32 * q + 3, :], sq_dram[:, q * (N // 4):(q + 1) * (N // 4)]).then_inc(sq_loaded, 16)
            pool.wait_ge(zl_ready, C + 2)
            pool.wait_ge(zh_ready, C)

            def low(item, k):
                pool.wait_ge(h_ready, item + k + 1)
                pool.tensor_tensor(itemL[:, k % HB], tcopy[:, k % 2], itemH[:, k % HB].bitcast(F32),
                                   ALU.subtract).then_inc(l_ready, 1)

            def double_z(t, par):
                for dst, src in ((z2H, zTH), (z2L, zTL)):
                    z = src[:, bass.ds(t * P, P)].bitcast(F32)
                    pool.tensor_tensor(dst[:, par], z, z, ALU.add).then_inc(z2_ready, 1)

            def carry_wait(j):
                pool.tensor_tensor(spare[:, j + 1:j + 2], spare[:, 0:1], spare[:, 0:1], ALU.add).then_inc(pool_step, 1)

            def load_hrow(half, j):
                if not isinstance(half, int) or half > 0:
                    pool.wait_ge(hs_stored, half * 16)
                    carry_wait(j)
                pool.dma_start(hrow[:, :, :], h_half[half]).then_inc(hrow_loaded, 16)

            def store_hrow(half, j):
                pool.wait_ge(hrow_made, half + 1)
                carry_wait(j)
                pool.dma_start(hs_half[half], hrow[:, :, :]).then_inc(hs_stored, 16)

            def load_stage(c):
                pool.wait_ge(hs_stored, c * 16 + 16)
                pool.wait_ge(hsh_ready, c * JT + HS2)
                pool.wait_ge(hsl_ready, c * JT + HS2)
                pool.dma_start(hs_stage[:, :, :], hs_chunk[c]).then_inc(stage_loaded, 16)

            def sim_tile(b, j, order, post, last=False):
                t = b * BLK + j
                item = (b - LAG) * ITEMS + (ITEM2 + j * 2 * JT)
                for what, k in order:
                    if what == "T":
                        low(item, k)
                        if j == 0 and k < JT:
                            pool.wait_ge(hsh_ready, (b - LAG) * JT + (HS2 + k + 1))
                            pool.tensor_tensor(hsL[:, k], hs_stage[:, k], hsH[:, k].bitcast(F32),
                                               ALU.subtract).then_inc(hsl_ready, 1)
                    if (what, k) == ("Z", 3) and not last:
                        if not isinstance(t, int) or t:
                            pool.wait_ge(zz_ready, t * NP)
                        double_z(t + 1, (j + 1) % 2)
                    if (what, k) == ("Z", 7) and post:
                        if j == 0:
                            load_hrow(b * 2 - 2, j)
                        if j == 5:
                            store_hrow(b * 2 - 2, j)
                        if j == 6:
                            load_hrow(b * 2 - 1, j)
                        if j == 7:
                            store_hrow(b * 2 - 1, j)
                if j == BLK - 1 and post:
                    load_stage(b - 1)

            def sim_block(b, order, post, last=False):
                for j in range(BLK):
                    sim_tile(b, j, order, post, last and j == BLK - 1)

            double_z(0, 0)
            sim_block(0, SIM_ONLY, False)
            sim_block(1, SIM_ONLY, True)
            with pool.Fori(LAG, NB - 1) as b:
                sim_block(b, ORDER, True)
            sim_block(NB - 1, ORDER, True, last=True)
            pool.wait_ge(top_found, T + 2)
            for half in range(2):
                pool.dma_start(hlast[:, half * HBK:(half + 1) * HBK],
                               h_half[2 * NB - 2 + half]).then_inc(hrow_loaded, 16)
            pool.wait_ge(hrow_made, 2 * NB - 1)
            for half in range(2):
                pool.dma_start(hs_half[2 * NB - 2 + half],
                               hlast[:, half * HBK:(half + 1) * HBK]).then_inc(hs_stored, 16)
            pool.wait_ge(hs_stored, 32 * NB)

            def fetch(t, e):
                pool.wait_ge(nbr_scaled, t + 1)
                pool.tensor_copy(idx[:, e], I4[:, bass.ds(t, 1), :].rearrange("p a k -> p (a k)")).then_inc(idx_ready, 1)
                pool.wait_ge(idx_ready, t + 1)
                carry_wait(0)
                for k in range(TOP):
                    pool.indirect_dma_start(
                        nbr[:, e * TOP + k], None, hs_dram,
                        bass.IndirectOffsetOnAxis(ap=idx[:, e, k:k + 1], axis=0)).then_inc(nbr_loaded[e], 16)

            def scale(t, qd, e):
                pool.wait_ge(nbr_loaded[e], qd * (16 * TOP) + 16 * TOP)
                pool.wait_ge(nsum_made, t + 1)
                pool.tensor_tensor(nbrs[:, e * TOP:(e + 1) * TOP], nbr[:, e * TOP:(e + 1) * TOP],
                                   S4[:, bass.ds(t, 1), :].rearrange("p a k -> p (a k)").unsqueeze(2)
                                   .to_broadcast([P, TOP, D]), ALU.mult).then_inc(nbr_scaled, 1)

            def quad_neighbours(qd, last=False):
                fetch(qd * 2 + 1, 1)
                scale(qd * 2, qd, 0)
                if not last:
                    fetch(qd * 2 + 2, 0)
                scale(qd * 2 + 1, qd, 1)

            pool.nop().then_inc(nbr_scaled, 2)
            fetch(0, 0)
            load_stage(C_SIM + 1)
            with pool.Fori(0, C_NBR - 1) as c:
                quad_neighbours(c * QUADS)
                load_stage(c + (C_SIM + 2))
                with pool.Fori(1, QUADS) as q:
                    quad_neighbours(c * QUADS + q)
            quad_neighbours((C_NBR - 1) * QUADS)
            load_stage(C_SIM + C_NBR + 1)
            with pool.Fori((C_NBR - 1) * QUADS + 1, C_NBR * QUADS - 1) as qd:
                quad_neighbours(qd)
            quad_neighbours(C_NBR * QUADS - 1, last=True)
            for c in range(C_SIM + C_NBR + 2, C):
                load_stage(c)

            pool.dma_start(w2s, W2).then_inc(w2_loaded, 16)
            pool.dma_start(b2bc, b2.partition_broadcast(P)).then_inc(w2_loaded, 16)
            pool.wait_ge(w2_loaded, 32)
            for k in range(RING):
                pool.wait_ge(x2_loaded[k], 16)
            with pool.Fori(0, C // 2) as gg:
                for e in range(2):
                    xg4 = xb[:, bass.ds(gg * (2 * JT) + e * JT, JT), :]
                    pool.tensor_tensor(xg4, xg4, b2bc.unsqueeze(1).to_broadcast([P, JT, D]),
                                       ALU.add).then_inc(xb_made, 1)

        @block.vector
        def _(dve):
            class Steps:
                base, n = 0, 0

            def step(ins):
                Steps.n += 1
                ins.then_inc(dve_step, 1)
                dve.wait_ge(dve_step, Steps.base + Steps.n)

            roots = [0]

            def rsqrt(dst, s, tmp, before):
                dve.reciprocal(tmp, s).then_inc(root_in, 1)
                dve.wait_ge(root_in, before + 1)
                dve.wait_ge(root_out, before + 1)
                newton(dst, s, tmp)

            def newton(dst, s, tmp):
                step(dve.tensor_tensor(tmp, dst, dst, ALU.mult))
                step(dve.tensor_tensor(tmp, tmp, s, ALU.mult))
                step(dve.tensor_scalar(tmp, tmp, -0.5, 1.5, ALU.mult, ALU.add))
                step(dve.tensor_tensor(dst, dst, tmp, ALU.mult))

            def per_row(ap, d):
                return ap.unsqueeze(2).to_broadcast([P, ap.shape[1], d])

            dve.nop().then_inc(acc_added, 2)
            dve.nop().then_inc(l_ready, 1)
            dve.nop().then_inc(z_made, 2)
            dve.nop().then_inc(zl_ready, 2)
            dve.nop().then_inc(o_made, 2)
            for k in range(RING):
                dve.nop().then_inc(summed[k], 1)
            for g in range(T // LNG):
                hg, part = h_all[:, g * LNG:(g + 1) * LNG], slice(g * LNG, (g + 1) * LNG)
                dve.wait_ge(x_loaded[g], 16)
                step(dve.reduce_sum(st[:, 0, part], hg, AX_X))
                step(dve.tensor_scalar(st[:, 0, part], st[:, 0, part], 1.0 / D, None, ALU.mult))
                step(dve.tensor_tensor(hg, hg, per_row(st[:, 0, part], D), ALU.subtract))
                step(dve.tensor_tensor(lt, hg, hg, ALU.mult))
                step(dve.reduce_sum(st[:, 1, part], lt, AX_X))
            step(dve.tensor_scalar(st[:, 1], st[:, 1], 1.0 / D, LN_EPS, ALU.mult, ALU.add))
            rsqrt(st[:, 3], st[:, 1], st[:, 2], 0)
            for g in range(T // LNG):
                hg = h_all[:, g * LNG:(g + 1) * LNG]
                step(dve.tensor_tensor(hg, hg, per_row(st[:, 3, g * LNG:(g + 1) * LNG], D), ALU.mult))
                dve.tensor_scalar(hg, hg, 0.0, None, ALU.max).then_inc(h_made, 1)
            step(dve.memset(acc[:, 0:RING * W], 0.0))

            def first_rows(s, R, q):
                item = (R * RING + q) * (s * JT) + ITEMS1[s]
                for k in range(RING):
                    for what in ("sum", "low") if sums_first(s) else ("low", "sum"):
                        if what == "low" and k < s:
                            for jt in range(JT):
                                dve.wait_ge(h_ready, item + (k * JT + jt + 1))
                                dve.tensor_tensor(itemL[:, jt], tbank[jt], itemH[:, jt].bitcast(F32),
                                                  ALU.subtract).then_inc(l_ready, 1)
                        if what == "sum" and k not in act_sums(s):
                            dve.wait_ge(a_loaded[k], (R * RING + q) * 16 + (s * BODIES * 16 + 16))
                            part = rs_part[:, bass.ds((R + s * RING) * JT, JT), bass.ds(q + k * RING, 1)]
                            dve.reduce_sum(part.rearrange("p a b -> p (a b)"), ring[:, k],
                                           AX_X).then_inc(summed[k], 1)

            for s in range(SUP):
                if s:
                    with dve.Fori(0, RING) as R:
                        with dve.Fori(0, RING) as q:
                            first_rows(s, R, q)
                        dve.wait_ge(m_done, (R + 1) * (RING * s * JT) + (ITEMS1[s] + HB))
                        dve.tensor_scalar(acc[:, bass.ds((R + s * RING) * W, W)], ab[0][:, :], 1.0, None,
                                          ALU.mult).then_inc(acc_added, 1)
                rows = slice(s * ST, (s + 1) * ST)
                for k in range(RING):
                    dve.wait_ge(summed[k], (s + 1) * BODIES + 1)
                step(dve.reduce_sum(rowsum[:, rows], rs_part[:, rows], AX_X))
                rsqrt(dinv[:, rows], rowsum[:, rows], rt[:, 0, rows], 1 + s)
                dve.wait_ge(h_stored, 16 * (T // LNG))
                dve.wait_ge(h_made, T // LNG)
                for g in range(s * ST // LNG, (s + 1) * ST // LNG):
                    hg = h_all[:, g * LNG:(g + 1) * LNG]
                    step(dve.tensor_tensor(hg, hg, per_row(dinv[:, g * LNG:(g + 1) * LNG], D), ALU.mult))
                dve.nop().then_inc(hs_made, 1)

            def add_group(bank, col, rg, done, sums=None):
                if sums is not None:
                    dve.wait_ge(nsum_added, sums + 2)
                dve.wait_ge(m_done, done + HB)
                dve.wait_ge(acc_added, rg + 2)
                dst = acc[:, bass.ds(col, W)]
                dve.tensor_tensor(dst, dst, ab[bank][:, :], ALU.add).then_inc(acc_added, 1)

            def split_quad(item, rg, col, prev_col, hs_src, nbr_qd=None, beside={}):
                for k in range(QI):
                    dve.wait_ge(h_ready, item + (k + 1))
                    dve.tensor_tensor(itemL[:, k % HB], tbank[k % 4], itemH[:, k % HB].bitcast(F32),
                                      ALU.subtract).then_inc(l_ready, 1)
                    if hs_src is not None and k < JT:
                        dve.wait_ge(hsh_ready, hs_src[1] + (k + 1))
                        dve.tensor_tensor(hsL[:, k], hs_src[0](k), hsH[:, k].bitcast(F32),
                                          ALU.subtract).then_inc(hsl_ready, 1)
                    if k % JT == 2:
                        r = k // JT
                        sums = None if nbr_qd is None else nbr_qd * 2 + int(k > 8)
                        if r:
                            add_group((r - 1) % 2, col + (r - 1) * W, rg + (r - 1), item + r * JT, sums)
                        elif prev_col is not None:
                            add_group((RING - 1) % 2, prev_col, rg - 1, item, sums)
                    if nbr_qd is not None and k in (4, 10):
                        e = int(k == 10)
                        t = nbr_qd * 2 + e
                        dve.wait_ge(nbr_scaled, t + 3)
                        dve.reduce_sum(nsum[:, e], nbrs[:, e * TOP:(e + 1) * TOP].rearrange("p k d -> p d k"),
                                       AX_X).then_inc(nsum_made, 1)
                    if nbr_qd is not None and k in (8, 14):
                        e = int(k == 14)
                        t = nbr_qd * 2 + e
                        dve.wait_ge(nsum_turned, t + 1)
                        dve.wait_ge(acc_added, rg + (3 + 2 * e))
                        dve.wait_ge(nsum_added, t + 2)
                        dst = acc[:, bass.ds(t * P, P)]
                        dve.tensor_tensor(dst, dst, nbank[e], ALU.add).then_inc(nsum_added, 1)
                    if k in beside:
                        beside[k]()

            def chunk(n, quads, rg, item, prev_col, hs_at, hs0, nbrs=False):
                rg, item, hs = n * (quads * RING) + rg, n * (quads * QI) + item, (hs_at, n * JT + hs0)
                split_quad(item, rg, 0, prev_col, hs, n * QUADS - QUADS if nbrs else None)
                if quads > 1:
                    with dve.Fori(1, quads) as q:
                        split_quad(item + q * QI, q * RING + rg, q * (RING * W), q * (RING * W) - W, None,
                                   q + n * QUADS - QUADS if nbrs else None)

            for s in range(SUP):
                run = (s + 1, RG1 + QUADS2[s] * RING, ITEMS1[SUP] + QUADS2[s] * QI)
                last_col = (s + 1) * (RING * W) - W
                hs_at = lambda c, k: h_all[:, bass.ds(c * JT + k, 1), :].rearrange("p a d -> p (a d)")
                hs0 = ITEMS1[SUP] + s * RING * JT
                c = s * RING
                chunk(0, *run, last_col - RING * W if s else None, (lambda k, c=c: hs_at(c, k)), hs0)
                with dve.Fori(1, RING) as n:
                    chunk(n, *run, last_col, lambda k: hs_at(n + s * RING, k), hs0)
            LASTCOL = (C - 1) * W
            add_group((RING - 1) % 2, LASTCOL, RG2 - 1, ITEM2)

            dve.wait_ge(w_loaded, 32)
            Steps.base, Steps.n = Steps.base + Steps.n, 0
            before = Steps.base
            with dve.Fori(0, C // 2) as gg:
                Steps.base, Steps.n = gg * 6 + before, 0
                for e in range(2):
                    g = gg * 2 + e
                    dve.wait_ge(us_ready, g + 3)
                    dve.tensor_scalar(acc[:, bass.ds(g * W, W)].rearrange("p (r d) -> p r d", d=P),
                                      ident[:, :].unsqueeze(1).to_broadcast([P, JT, P]), 0.0, None,
                                      ALU.mult).then_inc(dve_step, 1)
                    w3 = wt[:, e].rearrange("p (r d) -> p r d", d=D)
                    dve.wait_ge(ut_ready, g + 1)
                    Steps.n += 1
                    step(dve.tensor_tensor(w3, ab[e][:, :].rearrange("p (r d) -> p r d", d=D),
                                           per_row(dinv[:, bass.ds(g * JT, JT)], D), ALU.mult))
                    step(dve.tensor_tensor(w3, w3, b1bc.unsqueeze(1).to_broadcast([P, JT, D]), ALU.add))
                    dve.wait_ge(z_used, gg * (2 * JT) + 2 * JT)
                    dve.scalar_tensor_tensor(out=zt[:, e], in0=wt[:, e], scalar=SLOPE, in1=wt[:, e],
                                             op0=ALU.mult, op1=ALU.max).then_inc(z_made, 1)
                for e in range(2):
                    g = gg * 2 + e
                    dve.wait_ge(zh_ready, g + 1)
                    cols = bass.ds(g * W, W)
                    dve.tensor_tensor(zTL[:, cols], tb[e][:, :], zTH[:, cols].bitcast(F32),
                                      ALU.subtract).then_inc(zl_ready, 1)
            Steps.base, Steps.n = before + 6 * (C // 2), 0
            part = [sqp[:, k * T:(k + 1) * T] for k in range(3)]
            dve.wait_ge(z_used, T + 2 * JT)
            step(dve.tensor_copy(part[0], sq[:, :]))
            step(dve.tensor_tensor(sqr, sq[:, :], part[0], ALU.subtract))
            step(dve.tensor_copy(part[1], sqr))
            step(dve.tensor_tensor(sqr, sqr, part[1], ALU.subtract))
            step(dve.tensor_copy(part[2], sqr))
            dve.wait_ge(consts, 1)
            dve.tensor_copy(identb, ident[:, :]).then_inc(sqp_made, 1)
            for k in range(3):
                dve.wait_ge(sqt_ready, k + 1)
                dve.tensor_copy(sqt[0:T, k * P:(k + 1) * P],
                                [tb[0], tb[1], ab[0]][k][0:T, 0:P // 2].bitcast(BF16)).then_inc(sqt_copied, 1)

            dve.nop().then_inc(v_copied, 2)
            dve.nop().then_inc(top_found, 2)

            def sim_tile(b, j, product, last=False):
                t = b * BLK + j

                def add_groups():
                    for r in range(2):
                        g = 2 * j + r
                        add_group(r, g * W, (b - LAG) * C + (RG2 + g), (b - LAG) * ITEMS + (ITEM2 + (g + 1) * JT))

                if product and not last:
                    add_groups()
                dve.wait_ge(v_copied, t * NP + (NP + 2))
                dve.memset(spare[:, 1 + BLK:2 + BLK], 0.0).then_inc(dve_step, 1)
                dve.max(top8[:, j], v[:, j % 2]).then_inc(dve_step, 1)
                Steps.n += 2
                dve.wait_ge(dve_step, Steps.base + Steps.n)
                dve.memset(spare[:, 1 + BLK:2 + BLK], 0.0).then_inc(dve_step, 1)
                Steps.n += 1
                if last:
                    add_groups()
                dve.max_index(idx8[:, :], top8[:, j], v[:, j % 2]).then_inc(top_found, 1)
                dve.wait_ge(top_found, t + 3)
                step(dve.tensor_copy(I4[:, bass.ds(t, 1), :].rearrange("p a k -> p (a k)"), idx8[:, 0:TOP]))

            def distances(b):
                step(dve.tensor_tensor(dist[:, :, :], per_row(sq[:, bass.ds(b * BLK, BLK)], TOP),
                                       top8[:, :, 0:TOP], ALU.subtract))
                dve.tensor_scalar(dist[:, :, :], dist[:, :, :], 0.0, DIST_EPS,
                                  ALU.max, ALU.add).then_inc(dist_made, 1)

            def degrees(b):
                cols = bass.ds(b * BLK, BLK)
                dve.wait_ge(s_made, b + 1)
                step(dve.tensor_copy(S4[:, cols, :], dist[:, :, :]))
                step(dve.reduce_sum(rt[:, 1, 0:BLK], dist[:, :, :], AX_X))
                step(dve.tensor_tensor(rt[:, 1, 0:BLK], rt[:, 1, 0:BLK], rowsum[:, cols], ALU.add))
                dve.reciprocal(rt[:, 0, 0:BLK], rt[:, 1, 0:BLK]).then_inc(root_in, 1)

            def refine(b):
                dve.wait_ge(root_out, b + (ROOTS + 1))
                newton(rt[:, 1, BLK:2 * BLK], rt[:, 1, 0:BLK], rt[:, 0, 0:BLK])
                step(dve.tensor_copy(dinv[:, bass.ds(b * BLK, BLK)], rt[:, 1, BLK:2 * BLK]))

            def scale_hrow(b, half):
                dve.wait_ge(hrow_loaded, b * 32 + (half * 16 + 16))
                dve.tensor_tensor(hrow[:, :, :], hrow[:, :, :],
                                  per_row(dinv[:, bass.ds(b * BLK + half * HBK, HBK)], D),
                                  ALU.mult).then_inc(hrow_made, 1)

            def sim_block(b, product, post, last=False):
                for j in range(BLK):
                    if post and j == 2:
                        degrees(b - 1)
                    if post and j == 4:
                        refine(b - 1)
                        scale_hrow(b - 1, 0)
                    if post and j == 6:
                        scale_hrow(b - 1, 1)
                    sim_tile(b, j, product, last and j == BLK - 1)
                distances(b)

            sim_block(0, False, False)
            sim_block(1, False, True)
            start = Steps.base + Steps.n
            PER = 4 * BLK + 1 + 3 + 5
            with dve.Fori(LAG, NB - 1) as b:
                Steps.base, Steps.n = (b - LAG) * PER + start, 0
                sim_block(b, True, True)
                assert Steps.n == PER
            Steps.base, Steps.n = start + (NB - 1 - LAG) * PER, 0
            sim_block(NB - 1, True, True, last=True)

            def scale_hlast():
                dve.wait_ge(hrow_loaded, 32 * NB)
                dve.tensor_tensor(hlast, hlast, per_row(dinv[:, T - BLK:T], D), ALU.mult).then_inc(hrow_made, 1)

            def finish_degrees():
                refine(NB - 1)
                scale_hlast()

            dve.nop().then_inc(nsum_made, 2)
            dve.nop().then_inc(nsum_added, 2)
            hs_at = lambda k: hs_stage[:, k]
            hs5 = HS2 + C_SIM * JT
            for q in range(QUADS):
                split_quad(ITEM5 + q * QI, RG5 + q * RING, q * RING * W, q * RING * W - W if q else None,
                           None if q else (hs_at, hs5),
                           beside={0: {QI - 1: lambda: degrees(NB - 1)}, 1: {QI - 1: finish_degrees}}.get(q, {}))
            with dve.Fori(1, 1 + C_NBR) as n:
                chunk(n, QUADS, RG5, ITEM5, LASTCOL, hs_at, hs5, nbrs=True)
            with dve.Fori(1 + C_NBR, C - C_SIM) as n:
                chunk(n, QUADS, RG5, ITEM5, LASTCOL, hs_at, hs5)
            add_group((RING - 1) % 2, LASTCOL, RG2 + C * C - 1, 2 * ITEM2)

            with dve.Fori(0, C // 2) as gg:
                for e in range(2):
                    g = gg * 2 + e
                    o3 = ot[:, e * JT:(e + 1) * JT]
                    dve.wait_ge(o_ready, g + 3)
                    dve.wait_ge(out_stored[e], gg * 16 + 16)
                    dve.tensor_tensor(o3, ab[e][:, :].rearrange("p (r d) -> p r d", d=D),
                                      per_row(dinv[:, bass.ds(g * JT, JT)], D), ALU.mult).then_inc(o_scaled, 1)
                    dve.wait_ge(o_scaled, g + 1)
                    dve.wait_ge(xb_made, g + 1)
                    dve.tensor_tensor(o3, o3, xb[:, bass.ds(g * JT, JT), :], ALU.add).then_inc(o_made, 1)

        @block.tensor
        def _(pe):
            pe.nop().then_inc(t_ready, TR)
            pe.nop().then_inc(o_ready, 2)
            pe.nop().then_inc(m_done, HB)
            pe.wait_ge(consts, 1)

            def first_turn(s, m, item, body):
                k, jt = (m // JT) % s, m % JT
                if jt == 0:
                    pe.wait_ge(a_loaded[k], body * 16 + (16 * (m // (s * JT)) + s * BODIES * 16 + 16))
                if not isinstance(item, int) or item + m > 2:
                    pe.wait_ge(l_ready, item + (m - 2))
                for r in range(JT):
                    last = pe.transpose(tbank[jt][:, r * P:(r + 1) * P],
                                        ring[:, k, r, jt * P:(jt + 1) * P], ident[:, :])
                last.then_inc(t_ready, 1)

            def first_body(s, R, q, start=False, stop=False, last=False):
                body = R * RING + q
                item = body * (s * JT) + ITEMS1[s]
                for m in range(s * JT):
                    jt = m % JT
                    ahead = not (last and m + LEAD >= s * JT)
                    if ahead and s > 1:
                        first_turn(s, m + LEAD, item, body)
                    pe.wait_ge(l_ready, item + (m + 2))
                    if start and m == 0:
                        pe.wait_ge(acc_added, R + ((s - 1) * RING + 2))
                    pe.wait_ge(hsl_ready, item + (m + 1))
                    H, L, dst = itemH[:, jt], itemL[:, jt], ab[0][:, :]
                    pe.matmul(dst, hsH[:, jt], H, start=start and m == 0, stop=False)
                    pe.matmul(dst, hsH[:, jt], L, start=False, stop=False)
                    pe.matmul(dst, hsL[:, jt], H, start=False,
                              stop=stop and m == s * JT - 1).then_inc(m_done, 1)
                    if ahead and s == 1:
                        first_turn(s, m + LEAD, item, body)

            LEAD = 3
            for s in range(1, SUP):
                for m in range(LEAD):
                    first_turn(s, m, ITEMS1[s], 0)
                with pe.Fori(0, RING - 1) as R:
                    first_body(s, R, 0, start=True)
                    with pe.Fori(1, RING - 1) as q:
                        first_body(s, R, q)
                    first_body(s, R, RING - 1, stop=True)
                first_body(s, RING - 1, 0, start=True)
                with pe.Fori(1, RING - 1) as q:
                    first_body(s, RING - 1, q)
                first_body(s, RING - 1, RING - 1, stop=True, last=True)
            pe.wait_ge(acc_added, RG1 + 2)

            def turn(k, item, quads, free=True):
                slot, jt = (k // JT) % RING, k % JT
                if jt == 0:
                    pe.wait_ge(a_loaded[slot], quads * 16 + (16 * (k // QI) + 16))
                if free:
                    pe.wait_ge(l_ready, item + (k - 2))
                for r in range(JT):
                    last = pe.transpose(tbank[k % 4][:, r * P:(r + 1) * P],
                                        ring[:, slot, r, jt * P:(jt + 1) * P], ident[:, :])
                last.then_inc(t_ready, 1)

            def multiply(k, item, rg, hs_count):
                jt, bank = k % JT, (k // JT) % 2
                pe.wait_ge(l_ready, item + (k + 2))
                pe.wait_ge(h_ready, item + k + 1)
                if jt == 0:
                    pe.wait_ge(acc_added, rg + (k // JT + 1))
                if hs_count is not None:
                    pe.wait_ge(hsl_ready, hs_count + jt + 1)
                dst = ab[bank][:, :]
                H, L = itemH[:, k % HB], itemL[:, k % HB]
                pe.matmul(dst, hsH[:, jt], H, start=jt == 0, stop=False)
                pe.matmul(dst, hsH[:, jt], L, start=False, stop=False)
                pe.matmul(dst, hsL[:, jt], H, start=False, stop=jt == JT - 1).then_inc(m_done, 1)

            def quad(item, rg, quads, hs_count, last=False, nbr=None):
                for k in range(QI):
                    if k + LEAD < QI or not last:
                        turn(k + LEAD, item, quads)
                    multiply(k, item, rg, hs_count if k < JT else None)
                    if nbr is not None and k in (6, 12):
                        e = int(k == 12)
                        pe.wait_ge(nsum_made, nbr * 2 + (e + 3))
                        pe.wait_ge(nsum_added, nbr * 2 + (e + 1))
                        pe.transpose(nbank[e], nsum[:, e], ident[:, :]).then_inc(nsum_turned, 1)

            def product(runs, nbrs_of=0):
                for k in range(LEAD):
                    turn(k, runs[0][2], runs[0][4], free=False)
                for i, (n, quads, item0, rg0, load0, hs0, nbrs) in enumerate(runs):
                    def chunk(c, stop):
                        with pe.Fori(0, stop) as q:
                            quad(c * (quads * QI) + q * QI + item0, c * (quads * RING) + q * RING + rg0,
                                 c * quads + q + load0, c * JT + hs0, nbr=c * quads + q if nbrs else None)

                    end = i == len(runs) - 1
                    if n > end:
                        with pe.Fori(0, n - end) as c:
                            chunk(c, quads)
                    if end:
                        chunk(n - 1, quads - 1)
                        quad((n * quads - 1) * QI + item0, (n * quads - 1) * RING + rg0,
                             n * quads - 1 + load0, (n - 1) * JT + hs0, last=True)

            product([(RING, s + 1, ITEMS1[SUP] + QUADS2[s] * QI, RG1 + QUADS2[s] * RING,
                      SUP * BODIES + QUADS2[s], ITEMS1[SUP] + s * RING * JT, False) for s in range(SUP)])

            pe.wait_ge(acc_added, RG2 + 2)
            pe.wait_ge(w_loaded, 32)
            pe.wait_ge(l_ready, ITEM2 + 1)
            with pe.Fori(0, C // 2) as gg:
                for e in range(2):
                    g = gg * 2 + e
                    pe.wait_ge(us_ready, gg * 2 + 2)
                    pe.matmul(tbank[2 + e], w1s, acc[:, bass.ds(g * W, W)], start=True,
                              stop=True).then_inc(u_ready, 1)
                for e in range(2):
                    g = gg * 2 + e
                    pe.wait_ge(us_ready, g + 3)
                    pe.wait_ge(z_made, gg * 2 + 2)
                    for r in range(JT):
                        last = pe.transpose(ab[e][:, r * P:(r + 1) * P], us[:, e, r * P:(r + 1) * P], ident[:, :])
                    last.then_inc(ut_ready, 1)
                for e in range(2):
                    g = gg * 2 + e
                    pe.wait_ge(z_made, g + 3)
                    pe.wait_ge(zl_ready, gg * 2 + 2)
                    for r in range(JT):
                        last = pe.transpose(tb[e][:, r * P:(r + 1) * P], zt[:, e, r * P:(r + 1) * P], ident[:, :])
                    last.then_inc(zt_ready, 1)
            pe.wait_ge(sqp_made, 1)
            pe.wait_ge(zl_ready, C + 2)
            for k in range(3):
                pe.transpose([tb[0], tb[1], ab[0]][k][0:T, 0:P // 2].bitcast(BF16), sqp[:, k * T:(k + 1) * T],
                             identb).then_inc(sqt_ready, 1)

            pe.wait_ge(sqt_copied, 3)
            pe.wait_ge(sq_loaded, 64)
            pe.wait_ge(zh_ready, C)

            def sim_tile(b, j, par, order):
                t = b * BLK + j
                if len(order) > len(SIM_ONLY):
                    item, rg = (b - LAG) * ITEMS + (j * (2 * JT) + ITEM2), (b - LAG) * C + (j * 2 + RG2)
                pe.wait_ge(z2_ready, t * 2 + 2)
                for what, k in order:
                    if what == "T":
                        half, jt = (k // 2) % 2, k % 2
                        if jt == 0:
                            pe.wait_ge(ah_loaded[half], (b - LAG) * (16 * C) + (j * 32 + (16 * (k // JT) + 16)))
                        pe.wait_ge(t_copied, item + (k + 1 - ITEM2))
                        for r in range(JT):
                            last = pe.transpose(tb[k % 2][:, r * P:(r + 1) * P],
                                                ringh[:, half * JT + r, jt * P:(jt + 1) * P], ident[:, :])
                        last.then_inc(t_ready, 1)
                    if what == "M":
                        multiply(k, item, rg, (b - LAG) * JT + HS2)
                    if what == "Z":
                        pr, q = k // 2, k // 4
                        if k % 2 == 0:
                            pe.wait_ge(v_copied, t * NP + pr + 1)
                        dst = zz[pr % 2][:, (k % 2) * W:(k % 2 + 1) * W]
                        cols = slice(k * W, (k + 1) * W)
                        pe.matmul(dst, z2H[:, par], zTH[:, cols], start=True, stop=False)
                        pe.matmul(dst, z2H[:, par], zTL[:, cols], start=False, stop=False)
                        pe.matmul(dst, z2L[:, par], zTH[:, cols], start=False, stop=False)
                        last = pe.matmul(dst, negones[32 * q:32 * q + 3, :],
                                         sqrow[32 * q:32 * q + 3, (k % 4) * W:(k % 4 + 1) * W],
                                         start=False, stop=True)
                        if k % 2:
                            last.then_inc(zz_ready, 1)

            for b in range(LAG):
                with pe.Fori(0, BLK // 2) as pair:
                    for par in range(2):
                        sim_tile(b, pair * 2 + par, par, SIM_ONLY)
            with pe.Fori(LAG, NB - 1) as b:
                with pe.Fori(0, BLK // 2) as pair:
                    for par in range(2):
                        sim_tile(b, pair * 2 + par, par, ORDER)
            with pe.Fori(0, BLK // 2 - 1) as pair:
                for par in range(2):
                    sim_tile(NB - 1, pair * 2 + par, par, ORDER)
            sim_tile(NB - 1, BLK - 2, 0, ORDER)
            sim_tile(NB - 1, BLK - 1, 1, LAST_ORDER)

            pe.wait_ge(v_copied, T * NP + 2)
            pe.wait_ge(t_copied, C_SIM * ITEMS + 2)
            pe.wait_ge(l_ready, ITEM5 + 1)
            product([(n, QUADS, ITEM5 + c * ITEMS, RG5 + c * C, QUAD5 + c * QUADS, HS2 + (C_SIM + c) * JT, nbrs)
                     for c, n, nbrs in ((0, 1, False), (1, C_NBR, True), (1 + C_NBR, C - C_SIM - C_NBR - 1, False))])

            pe.wait_ge(acc_added, RG2 + C * C + 2)
            pe.wait_ge(w2_loaded, 32)
            with pe.Fori(0, C // 2) as gg:
                for e in range(2):
                    g = gg * 2 + e
                    pe.wait_ge(accs_ready, g + 1)
                    pe.wait_ge(o_made, gg * 2 + 2)
                    for r in range(JT):
                        last = pe.matmul(ab[e][:, r * P:(r + 1) * P], accs[:, e, r * P:(r + 1) * P], w2s,
                                         start=True, stop=True)
                    last.then_inc(o_ready, 1)


_INS = ["x", "adj", "L0_gnn_W1", "L0_gnn_b1", "L0_gnn_W2", "L0_gnn_b2"]


def kernel(**inputs):
    import numpy as np
    import concourse.bacc as bacc
    from concourse.bass_utils import run_bass_kernel_spmd

    nc = bacc.Bacc("TRN2", target_bir_lowering=False, num_devices=1)
    arrays, args = {}, []
    for name in _INS:
        a = np.ascontiguousarray(inputs[name])
        arrays[name + "_in"] = a
        args.append(nc.dram_tensor(name + "_in", a.shape, mybir.dt.from_np(a.dtype), kind="ExternalInput").ap())
    out = nc.dram_tensor("out", inputs["x"].shape, F32, kind="ExternalOutput").ap()
    gnn_kernel(nc, *args, out)
    r = run_bass_kernel_spmd(nc, [arrays], core_ids=[0])
    return r.results[0]["out"]
```

```python
from contextlib import ExitStack

import concourse.bass as bass
from concourse import mybir

F32 = mybir.dt.float32
F32R = mybir.dt.float32r
BF16 = mybir.dt.bfloat16
U32 = mybir.dt.uint32
ACT = mybir.ActivationFunctionType
ALU = mybir.AluOpType
AX_X = mybir.AxisListType.X

P = 128
LN_EPS = 1e-5
DIST_EPS = 1e-10
SLOPE = 0.1
ACT_ORDERS = ("S0 S1 S2 S3",
              "H0 H1 H2 H3 S2 S3",
              "H0 H1 H2 H3 H4 H5 H6 H7 S3",
              "H0 H1 H2 H3 R0 H4 H5 H6 H7 R1 H8 H9 H10 H11 S3")
DVE_ORDERS = ("",
              "S0 L0 L1 S1 L2 L3",
              "S0 L0 L1 S1 L2 L3 S2 L4 L5 L6 L7",
              "L0 L1 L2 L3 S0 L4 L5 L6 L7 S1 L8 L9 L10 L11 S2")
TOP = 4
W = 512
JT = W // P
HB = 4
RING = 4
BLK = 8
OB = 4
LAG = 2


def gnn_kernel(nc, x, adj, W1, b1, W2, b2, out):
    N, D = x.shape
    T = N // P
    C = N // W
    QUADS = C // RING
    ITEMS = C * JT
    QI = RING * JT
    SUP = C // RING
    ST = T // SUP
    BODIES = RING * RING
    ITEMS1 = [sum(BODIES * r * JT for r in range(s)) for s in range(SUP + 1)]
    QUADS2 = [sum(RING * (r + 1) for r in range(s)) for s in range(SUP + 1)]
    NB = T // BLK
    C_SIM = NB - LAG
    LNG = 8
    ZP = 2 * W
    NP = N // ZP
    HALF = W // 2

    ctx = ExitStack()
    with ctx:
        def sb(name, shape, dt=F32):
            return ctx.enter_context(nc.sbuf_tensor(name, shape, dt))

        def sem(name):
            return ctx.enter_context(nc.semaphore(name))

        acc = sb("acc", [P, N])
        zTH = sb("zTH", [P, N], F32R)
        zTL = sb("zTL", [P, N], F32R)
        itemH = sb("itemH", [P, HB, W], F32R)
        itemL = sb("itemL", [P, HB, W], F32R)
        hsH = sb("hsH", [P, JT, D], F32R)
        hsL = sb("hsL", [P, JT, D], F32R)
        z2H = sb("z2H", [P, 2, P], F32R)
        z2L = sb("z2L", [P, 2, P], F32R)
        ident = sb("ident", [P, P])
        negones = sb("negones", [P, P], BF16)
        rowsum = sb("rowsum", [P, T])
        dinv = sb("dinv", [P, T])
        sq = sb("sq", [P, T])
        S4 = sb("S4", [P, T, TOP])
        I4 = sb("I4", [P, T, TOP], U32)
        idx8 = sb("idx8", [P, 8], U32)
        top8 = sb("top8", [P, BLK, 8])
        dist = sb("dist", [P, BLK, TOP])
        hs_stage = sb("hs_stage", [P, JT, D])
        hrow = sb("hrow", [P, BLK // 2, D])
        ARENA = 20480
        HBK = BLK // 2
        arena = sb("arena", [P, ARENA])

        def view(at, *shape):
            n = 1
            for s in shape:
                n *= s
            assert at + n <= ARENA
            v = arena[:, at:at + n]
            if len(shape) == 2:
                v = v.rearrange("p (a b) -> p a b", b=shape[1])
            if len(shape) == 3:
                v = v.rearrange("p (a b c) -> p a b c", b=shape[1], c=shape[2])
            return v

        ring = view(0, RING, JT, W)
        RINGW = RING * JT * W
        h_all = view(RINGW, T, D)
        lt = view(RINGW + T * D, LNG, D)
        st = view(RINGW + T * D + LNG * D, 4, T)
        rs_part = view(RINGW + T * D + LNG * D + 4 * T, T, C)
        sumjunk = view(RINGW + T * D, 2, W)
        F3 = RINGW + T * D
        w1s = view(F3, D)
        b1bc = view(F3 + D, D)
        us = view(F3 + 2 * D, 2, W)
        wt = view(F3 + 2 * D + 2 * W, 2, W)
        zt = view(F3 + 2 * D + 4 * W, 2, W)
        zjunk = view(0, 2, W)
        sqr = view(2 * W, T)
        sqp = view(2 * W + T, 3 * T // 2).bitcast(BF16)
        sqt = view(2 * W + T + 3 * T // 2, 3 * P // 2).bitcast(BF16)
        identb = view(2 * W + 4 * T + 2 * P, P // 2).bitcast(BF16)
        v = view(0, 2, N)
        ringh = view(2 * N, 2 * JT, HALF)
        tcopy = view(2 * N + 2 * JT * HALF, 2, W)
        sqrow = view(2 * N + 2 * JT * HALF + 2 * W, N // 8).bitcast(BF16)
        nbr = view(RINGW, 2 * TOP, D)
        nbrs = view(RINGW + 2 * TOP * D, 2 * TOP, D)
        nsum = view(RINGW + 4 * TOP * D, 2, D)
        hlast = view(RINGW + 4 * TOP * D + 2 * D, BLK, D)
        ot = view(RINGW, OB, JT, D)
        accs = view(RINGW + 4 * TOP * D + 2 * D, 2, W)
        F6 = RINGW + 4 * TOP * D + 2 * D + BLK * D
        w2s = view(F6, D)
        b2bc = view(F6 + D, D)
        xb = view(F6 + 2 * D, T, D)
        idx = sb("idx", [P, 2, TOP], U32)
        rt = sb("rt", [P, 2, T])
        spare = sb("spare", [P, 2 + BLK])

        tb = [ctx.enter_context(nc.psum_tensor(f"tb{i}", [P, W], F32)) for i in range(2)]
        ab = [ctx.enter_context(nc.psum_tensor(f"ab{i}", [P, W], F32)) for i in range(2)]
        zz = [ctx.enter_context(nc.psum_tensor(f"zz{i}", [P, ZP], F32)) for i in range(2)]
        tbank = [tb[0][:, :], tb[1][:, :], zz[0][:, 0:W], zz[0][:, W:ZP]]
        obank = [ab[0][:, :], ab[1][:, :], tbank[0], tbank[1]]
        nbank = [zz[1][:, 0:P], zz[1][:, W:W + P]]

        h_dram = nc.dram_tensor("h_dram", (N, D), F32, kind="Internal").ap()
        hs_dram = nc.dram_tensor("hs_dram", (N, D), F32, kind="Internal").ap()
        sq_dram = nc.dram_tensor("sq_dram", (3, N), BF16, kind="Internal").ap()

        A_groups = adj.rearrange("(g r p) (c w) -> g c p r w", r=JT, p=P, w=W)
        A_halves = adj.rearrange("(g r p) (c e w) -> g c e p r w", r=JT, p=P, e=2, w=HALF)
        x_ln = x.rearrange("(g t p) d -> g p t d", t=LNG, p=P)
        h_ln = h_dram.rearrange("(g t p) d -> g p t d", t=LNG, p=P)
        h_half = h_dram.rearrange("(g t p) d -> g p t d", t=HBK, p=P)
        hs_half = hs_dram.rearrange("(g t p) d -> g p t d", t=HBK, p=P)
        hs_chunk = hs_dram.rearrange("(c t p) d -> c p t d", t=JT, p=P)
        x_slot = x.rearrange("(k t p) d -> k p t d", t=T // RING, p=P)
        out_v = out.rearrange("(g t p) d -> g p t d", t=JT, p=P)

        consts = sem("consts")
        x_loaded = [sem(f"x_loaded{i}") for i in range(T // LNG)]
        h_made = sem("h_made")
        h_stored = sem("h_stored")
        summed = [sem(f"summed{i}") for i in range(RING)]
        last_summed = [sem(f"last_summed{i}") for i in range(RING)]
        root_in = sem("root_in")
        root_out = sem("root_out")
        dve_step = sem("dve_step")
        act_step = sem("act_step")
        pool_step = sem("pool_step")
        hs_made = sem("hs_made")
        a_loaded = [sem(f"a_loaded{i}") for i in range(RING)]
        t_ready = sem("t_ready")
        h_ready = sem("h_ready")
        l_ready = sem("l_ready")
        t_copied = sem("t_copied")
        m_done = sem("m_done")
        acc_added = sem("acc_added")
        hsh_ready = sem("hsh_ready")
        hsl_ready = sem("hsl_ready")
        stage_loaded = sem("stage_loaded")
        ah_loaded = [sem(f"ah_loaded{i}") for i in range(2)]

        w_loaded = sem("w_loaded")
        w2_loaded = sem("w2_loaded")
        u_ready = sem("u_ready")
        us_ready = sem("us_ready")
        ut_ready = sem("ut_ready")
        w_made = sem("w_made")
        b_added = sem("b_added")
        acc_cleared = sem("acc_cleared")
        z_made = sem("z_made")
        z_used = sem("z_used")
        zt_ready = sem("zt_ready")
        zh_ready = sem("zh_ready")
        zl_ready = sem("zl_ready")
        sqp_made = sem("sqp_made")
        sqt_ready = sem("sqt_ready")
        sqt_copied = sem("sqt_copied")
        sq_stored = sem("sq_stored")
        sq_loaded = sem("sq_loaded")
        z2_ready = sem("z2_ready")
        zz_ready = sem("zz_ready")
        v_copied = sem("v_copied")
        top_found = sem("top_found")
        dist_made = sem("dist_made")
        s_made = sem("s_made")
        hrow_loaded = sem("hrow_loaded")
        hrow_made = sem("hrow_made")
        hs_stored = sem("hs_stored")
        nbr_loaded = [sem(f"nbr_loaded{i}") for i in range(2)]
        idx_ready = sem("idx_ready")
        nbr_scaled = sem("nbr_scaled")
        nsum_made = sem("nsum_made")
        nsum_turned = sem("nsum_turned")
        nsum_added = sem("nsum_added")
        accs_ready = sem("accs_ready")
        o_ready = sem("o_ready")
        o_scaled = sem("o_scaled")
        o_made = sem("o_made")
        x2_loaded = [sem(f"x2_loaded{i}") for i in range(RING)]
        xb_made = sem("xb_made")
        out_stored = [sem(f"out_stored{i}") for i in range(OB)]

        TR = (RING - 1) * JT + 1
        ITEM2 = C * ITEMS
        RG1 = (SUP - 1) * RING
        RG2 = RG1 + QUADS2[SUP] * RING
        QUAD5 = SUP * BODIES + QUADS2[SUP]
        HS2 = ITEMS1[SUP] + C * JT
        ROOTS = 1 + SUP
        ITEM5 = ITEM2 + C_SIM * ITEMS
        RG5 = RG2 + C_SIM * C
        C_NBR = T // (2 * QUADS)
        LEAD = 3

        def parse(order):
            return [(w[0], int(w[1:])) for w in order.split()]

        ACT1, DVE1 = [[parse(order) for order in orders] for orders in (ACT_ORDERS, DVE_ORDERS)]

        def shared(s, k):
            return ("R", k) in ACT1[s]

        def first_shared(k):
            return min(s for s in range(SUP) if shared(s, k))

        ORDER = ("T0 T1 Z0 Z1 Z2 T2 M0 Z3 Z4 T3 M1 Z5 Z6 T4 M2 Z7 Z8 T5 M3 Z9 Z10 T6 M4 Z11 T7 M5 "
                 "Z12 Z13 M6 Z14 Z15 M7")
        LAST_ORDER = ("T0 T1 Z0 Z1 Z2 Z3 Z4 Z5 Z6 Z7 Z8 Z9 Z10 Z11 Z12 Z13 Z14 Z15 T2 M0 T3 M1 T4 M2 "
                      "T5 M3 T6 M4 T7 M5 M6 M7")
        ORDER, LAST_ORDER = parse(ORDER), parse(LAST_ORDER)
        SIM_ONLY = [s for s in ORDER if s[0] == "Z"]

        block = ctx.enter_context(nc.Block())

        def pipeline(engine, stages):
            for g in range(-max(ahead for ahead, _ in stages), 0):
                for ahead, stage in stages:
                    if g + ahead >= 0:
                        stage(g + ahead, (g + ahead) % 2)
            with engine.Fori(0, C // 2 - 2) as gg:
                for e in range(2):
                    for ahead, stage in stages:
                        stage(gg * 2 + (e + ahead), (e + ahead) % 2)
            for g in range(C - 4, C):
                for ahead, stage in stages:
                    if g + ahead < C:
                        stage(g + ahead, (g + ahead) % 2)

        @block.sync
        def _(sp):
            for e in range(OB):
                sp.nop().then_inc(out_stored[e], 16)
            for s in range(SUP):
                if s > 1:
                    sp.wait_ge(t_ready, ITEMS1[s] + TR)
                with sp.Fori(0, RING) as R:
                    with sp.Fori(0, RING) as q:
                        for k in range(RING):
                            loads = R * RING + q + (s * BODIES + 1)
                            if k < s:
                                sp.wait_ge(t_ready, R * (RING * s * JT) + q * (s * JT)
                                           + (ITEMS1[s] + TR - (s - 1 - k) * JT))
                            if shared(s, k):
                                sp.wait_ge(last_summed[k], loads)
                            sp.wait_ge(summed[k], loads)
                            sp.dma_start(ring[:, k], A_groups[R + s * RING, q + k * RING]).then_inc(a_loaded[k], 16)
            sp.wait_ge(t_ready, ITEMS1[SUP] + TR)
            for k in range(RING):
                sp.wait_ge(summed[k], SUP * BODIES + 1)
                if shared(SUP - 1, k):
                    sp.wait_ge(last_summed[k], SUP * BODIES + 1)

            def load_groups(c0, c1, quads, item0):
                with sp.Fori(c0, c1) as c:
                    with sp.Fori(0, quads) as q:
                        for k in range(RING):
                            sp.wait_ge(t_ready, (c - c0) * (quads * QI) + q * QI + (item0 + k * JT + 1))
                            sp.dma_start(ring[:, k], A_groups[q * RING + k, c]).then_inc(a_loaded[k], 16)

            for s in range(SUP):
                load_groups(s * RING, (s + 1) * RING, s + 1, ITEMS1[SUP] + QUADS2[s] * QI)

            sp.wait_ge(sqt_copied, 3)
            sp.dma_start(sq_dram.rearrange("k (t p) -> t k p", p=P),
                         sqt[0:T, :].rearrange("t (k p) -> t k p", p=P)).then_inc(sq_stored, 16)
            sp.wait_ge(sq_stored, 16)
            for q in range(4):
                sp.dma_start(sqrow[32 * q:32 * q + 3, :],
                             sq_dram[:, q * (N // 4):(q + 1) * (N // 4)]).then_inc(sq_loaded, 16)

            with sp.Fori(0, C_SIM) as c:
                with sp.Fori(0, C) as g:
                    for e in range(2):
                        sp.wait_ge(t_ready, c * ITEMS + g * JT + (ITEM2 + TR + (JT // 2) * (e - 1)))
                        sp.dma_start(ringh[:, e * JT:e * JT + JT], A_halves[g, c, e]).then_inc(ah_loaded[e], 16)
            sp.wait_ge(top_found, T + 1)
            load_groups(C_SIM, C, QUADS, ITEM5)
            with sp.Fori(0, C // OB) as gg:
                for e in range(OB):
                    sp.wait_ge(o_made, gg * OB + (e + 1))
                    sp.dma_start(out_v[gg * OB + e], ot[:, e]).then_inc(out_stored[e], 16)
            for e in range(OB):
                sp.wait_ge(out_stored[e], 16 * (C // OB) + 16)

        @block.scalar
        def _(act):
            act.nop().then_inc(us_ready, 2)
            act.nop().then_inc(z_used, 2 * JT)
            roots = [0]

            def root(dst, src):
                act.wait_ge(root_in, roots[0] + 1)
                act.activation(dst, src, ACT.Sqrt).then_inc(root_out, 1)
                roots[0] += 1

            def hs_tile(tile):
                return h_all[:, bass.ds(tile, 1), :].rearrange("p a d -> p (a d)")

            def sum_rows(k, s, R, q, rows, done):
                act.wait_ge(a_loaded[k], (R * RING + q) * 16 + (s * BODIES * 16 + 16))
                for r in rows:
                    part = rs_part[:, bass.ds((R + s * RING) * JT + r, 1), bass.ds(q + k * RING, 1)]
                    dst = ring[:, k, r]
                    if k < s:
                        act.wait_ge(done, (R * RING + q) + (s * BODIES + 1))
                        dst = sumjunk[:, k]
                    last = act.activation(dst, ring[:, k, r], ACT.Copy,
                                          accum_out=part.rearrange("p a b -> p (a b)"))
                last.then_inc(done, 1)

            def first_rows(s, R, q):
                item = (R * RING + q) * (s * JT) + ITEMS1[s]
                for what, k in ACT1[s]:
                    if what == "H":
                        jt = k % JT
                        act.wait_ge(t_ready, item + (k + 1 + TR))
                        act.wait_ge(m_done, item + (k + 1))
                        act.activation(itemH[:, jt], tbank[jt], ACT.Copy).then_inc(h_ready, 1)
                        act.activation(hsH[:, jt], hs_tile((q + (k // JT) * RING) * JT + jt),
                                       ACT.Copy).then_inc(hsh_ready, 1)
                    if what == "S":
                        sum_rows(k, s, R, q, range(JT), summed[k])
                    if what == "R":
                        sum_rows(k, s, R, q, (JT - 1,), last_summed[k])

            for s in range(SUP):
                if s:
                    act.wait_ge(hs_made, s)
                if s == 0:
                    with act.Fori(0, RING) as q:
                        first_rows(0, 0, q)
                    root(st[:, 3], st[:, 2])
                with act.Fori(1 if s == 0 else 0, RING) as R:
                    with act.Fori(0, RING) as q:
                        first_rows(s, R, q)
                root(dinv[:, s * ST:(s + 1) * ST], rt[:, 0, s * ST:(s + 1) * ST])
            act.wait_ge(hs_made, SUP)

            def split_quad(item, first, hs_src, beside={}):
                for k in range(QI):
                    act.wait_ge(t_ready, item + (k + 1 + TR))
                    act.wait_ge(m_done, item + k + 1)
                    act.activation(itemH[:, k % HB], tbank[k % 4], ACT.Copy).then_inc(h_ready, 1)
                    if first and k < JT:
                        act.activation(hsH[:, k], hs_src(k), ACT.Copy).then_inc(hsh_ready, 1)
                    if k in beside:
                        beside[k]()

            for s in range(SUP):
                with act.Fori(s * RING, (s + 1) * RING) as c:
                    item = (c - s * RING) * ((s + 1) * QI) + (ITEMS1[SUP] + QUADS2[s] * QI)
                    split_quad(item, True, lambda k: hs_tile(c * JT + k))
                    if s:
                        with act.Fori(1, s + 1) as q:
                            split_quad(item + q * QI, False, None)

            def copy_u(g, e):
                act.wait_ge(u_ready, g + 1)
                if not isinstance(g, int) or g > 1:
                    act.wait_ge(ut_ready, g - 1)
                act.activation(us[:, e], tbank[2 + e], ACT.Copy).then_inc(us_ready, 1)

            def square_z(g, e):
                act.wait_ge(z_used, g * JT + JT)
                act.wait_ge(z_made, g + 3)
                for r in range(JT):
                    act.activation(zjunk[:, e, r * P:(r + 1) * P], zt[:, e, r * P:(r + 1) * P], ACT.Square,
                                   accum_out=sq[:, bass.ds(g * JT + r, 1)]).then_inc(z_used, 1)

            def copy_z(g, e):
                act.wait_ge(zt_ready, g + 1)
                act.activation(zTH[:, bass.ds(g * W, W)], tb[e][:, :], ACT.Copy).then_inc(zh_ready, 1)

            pipeline(act, ((3, copy_u), (0, copy_z), (0, square_z)))

            act.nop().then_inc(t_copied, 2)

            def sim_tile(t, par, order, item, hs_count=None):
                for what, k in order:
                    if what == "T":
                        act.wait_ge(t_ready, item + (k + 1 + TR))
                        act.wait_ge(l_ready, item + k)
                        act.activation(tcopy[:, k % 2], tb[k % 2][:, :], ACT.Copy).then_inc(t_copied, 1)
                        act.wait_ge(m_done, item + k + 1)
                        act.wait_ge(t_copied, item + (k + 3 - ITEM2))
                        act.activation(itemH[:, k % HB], tcopy[:, k % 2], ACT.Copy).then_inc(h_ready, 1)
                        if hs_count is not None and k < JT:
                            act.wait_ge(stage_loaded, hs_count)
                            act.activation(hsH[:, k], hs_stage[:, k], ACT.Copy).then_inc(hsh_ready, 1)
                    if what == "Z" and k % 2:
                        pr = k // 2
                        if pr == 0:
                            act.wait_ge(top_found, t + 1)
                        act.wait_ge(zz_ready, t * NP + pr + 1)
                        act.activation(v[:, par, pr * ZP:(pr + 1) * ZP], zz[pr % 2][:, :],
                                       ACT.Copy).then_inc(v_copied, 1)

            def sim_pair(b, pair, order, last=False):
                for par in range(2):
                    t = b * BLK + (2 * pair + par)
                    sim_tile(t, par, LAST_ORDER if last and par else order,
                             (b - LAG) * ITEMS + (ITEM2 + (2 * pair + par) * 2 * JT),
                             (b - LAG) * 16 + 16 if pair == 0 and par == 0 else None)

            def similarities(b):
                act.wait_ge(dist_made, b + 1)
                act.activation(dist[:, :, :], dist[:, :, :], ACT.Sqrt).then_inc(act_step, 1)
                act.wait_ge(act_step, b + 1)
                act.activation(dist[:, :, :], dist[:, :, :], ACT.Exp, scale=-0.5).then_inc(s_made, 1)

            def block_root(b):
                act.wait_ge(root_in, b + (roots[0] + 1))
                act.activation(rt[:, 1, BLK:2 * BLK], rt[:, 0, 0:BLK], ACT.Sqrt).then_inc(root_out, 1)

            def sim_block(b, order, post, last=False):
                sim_pair(b, 0, order)
                if post:
                    similarities(b - 1)
                sim_pair(b, 1, order)
                if post:
                    block_root(b - 1)
                sim_pair(b, 2, order)
                sim_pair(b, 3, order, last)



            sim_block(0, SIM_ONLY, False)
            sim_block(1, SIM_ONLY, True)
            with act.Fori(LAG, NB - 1) as b:
                sim_block(b, ORDER, True)
            sim_block(NB - 1, ORDER, True, last=True)

            act.wait_ge(stage_loaded, C_SIM * 16 + 16)
            split_quad(ITEM5, True, lambda k: hs_stage[:, k], {JT - 1: lambda: similarities(NB - 1)})
            split_quad(ITEM5 + QI, False, None, {QI // 2: lambda: block_root(NB - 1)})
            for q in range(2, QUADS):
                split_quad(ITEM5 + q * QI, False, None)
            with act.Fori(C_SIM + 1, C) as c:
                act.wait_ge(stage_loaded, c * 16 + 16)
                split_quad((c - C_SIM) * ITEMS + ITEM5, True, lambda k: hs_stage[:, k])
                with act.Fori(1, QUADS) as q:
                    split_quad((c - C_SIM) * ITEMS + q * QI + ITEM5, False, None)

            act.wait_ge(acc_added, RG2 + C * C + 2)
            act.wait_ge(nsum_added, T + 2)
            act.wait_ge(m_done, 2 * ITEM2 + HB)
            with act.Fori(0, C // 2) as gg:
                for e in range(2):
                    g = gg * 2 + e
                    act.wait_ge(o_ready, g + 1)
                    act.activation(accs[:, e], acc[:, bass.ds(g * W, W)], ACT.Copy).then_inc(accs_ready, 1)

        @block.gpsimd
        def _(pool):
            steps = [0]

            def step(ins):
                steps[0] += 1
                ins.then_inc(pool_step, 1)
                pool.wait_ge(pool_step, steps[0])

            for g in range(T // LNG):
                pool.dma_start(h_all[:, g * LNG:(g + 1) * LNG], x_ln[g]).then_inc(x_loaded[g], 16)
            step(pool.memset(ident[:, :], 0.0))
            step(pool.affine_select(out=ident[:, :], in_=ident[:, :], compare_op=ALU.not_equal, fill=1.0,
                                    base=0, pattern=[[-1, P]], channel_multiplier=1))
            step(pool.memset(negones[:, :], -1.0))
            step(pool.memset(spare[:, 0:1], 0.0))
            pool.nop().then_inc(consts, 1)
            for g in range(T // LNG):
                pool.wait_ge(h_made, g + 1)
                pool.dma_start(h_ln[g], h_all[:, g * LNG:(g + 1) * LNG]).then_inc(h_stored, 16)
            for s in range(1, SUP):
                pool.wait_ge(hs_made, s)
                with pool.Fori(0, RING) as R:
                    with pool.Fori(0, RING) as q:
                        for m in range(s * JT):
                            k, jt = m // JT, m % JT
                            tile = h_all[:, bass.ds(q * JT + (k * RING * JT + jt), 1), :]
                            pool.wait_ge(hsh_ready, R * (RING * s * JT) + q * (s * JT) + (ITEMS1[s] + m + 1))
                            pool.tensor_tensor(hsL[:, jt], tile.rearrange("p a d -> p (a d)"),
                                               hsH[:, jt].bitcast(F32), ALU.subtract).then_inc(hsl_ready, 1)

            pool.wait_ge(hs_made, SUP)
            pool.dma_start(w1s, W1).then_inc(w_loaded, 16)
            pool.dma_start(b1bc, b1.partition_broadcast(P)).then_inc(w_loaded, 16)
            pool.wait_ge(w_loaded, 32)
            with pool.Fori(0, C // 2) as gg:
                for e in range(2):
                    w3 = wt[:, e].rearrange("p (r d) -> p r d", d=D)
                    pool.wait_ge(w_made, gg * 2 + e + 3)
                    pool.tensor_tensor(w3, w3, b1bc.unsqueeze(1).to_broadcast([P, JT, D]),
                                       ALU.add).then_inc(b_added, 1)
            pool.wait_ge(u_ready, C)
            pool.memset(acc[:, :], 0.0).then_inc(acc_cleared, 1)
            pool.wait_ge(h_stored, 16 * (T // LNG))
            pool.wait_ge(zl_ready, C + 2)
            pool.wait_ge(zh_ready, C)

            def low(item, k):
                pool.wait_ge(h_ready, item + k + 1)
                pool.tensor_tensor(itemL[:, k % HB], tcopy[:, k % 2], itemH[:, k % HB].bitcast(F32),
                                   ALU.subtract).then_inc(l_ready, 1)

            def double_z(t, par):
                for dst, src in ((z2H, zTH), (z2L, zTL)):
                    z = src[:, bass.ds(t * P, P)].bitcast(F32)
                    pool.tensor_tensor(dst[:, par], z, z, ALU.add).then_inc(z2_ready, 1)

            def carry_wait(j):
                pool.tensor_tensor(spare[:, j + 1:j + 2], spare[:, 0:1], spare[:, 0:1],
                                   ALU.add).then_inc(pool_step, 1)

            def load_hrow(half, j):
                if not isinstance(half, int) or half > 0:
                    pool.wait_ge(hs_stored, half * 16)
                    carry_wait(j)
                pool.dma_start(hrow[:, :, :], h_half[half]).then_inc(hrow_loaded, 16)

            def store_hrow(half, j):
                pool.wait_ge(hrow_made, half + 1)
                carry_wait(j)
                pool.dma_start(hs_half[half], hrow[:, :, :]).then_inc(hs_stored, 16)

            def load_stage(c):
                pool.wait_ge(hs_stored, c * 16 + 16)
                pool.wait_ge(hsh_ready, c * JT + HS2)
                pool.wait_ge(hsl_ready, c * JT + HS2)
                pool.dma_start(hs_stage[:, :, :], hs_chunk[c]).then_inc(stage_loaded, 16)

            def sim_tile(b, j, order, post, last=False):
                t = b * BLK + j
                item = (b - LAG) * ITEMS + (ITEM2 + j * 2 * JT)
                for what, k in order:
                    if what == "T":
                        low(item, k)
                        if j == 0 and k < JT:
                            pool.wait_ge(hsh_ready, (b - LAG) * JT + (HS2 + k + 1))
                            pool.tensor_tensor(hsL[:, k], hs_stage[:, k], hsH[:, k].bitcast(F32),
                                               ALU.subtract).then_inc(hsl_ready, 1)
                    if (what, k) == ("Z", 3) and not last:
                        if not isinstance(t, int) or t:
                            pool.wait_ge(zz_ready, t * NP)
                        double_z(t + 1, (j + 1) % 2)
                    if (what, k) == ("Z", 7) and post:
                        if j == 0:
                            load_hrow(b * 2 - 2, j)
                        if j == 5:
                            store_hrow(b * 2 - 2, j)
                        if j == 6:
                            load_hrow(b * 2 - 1, j)
                        if j == 7:
                            store_hrow(b * 2 - 1, j)
                if j == BLK - 1 and post:
                    load_stage(b - 1)

            def sim_block(b, order, post, last=False):
                for j in range(BLK):
                    sim_tile(b, j, order, post, last and j == BLK - 1)

            double_z(0, 0)
            sim_block(0, SIM_ONLY, False)
            sim_block(1, SIM_ONLY, True)
            with pool.Fori(LAG, NB - 1) as b:
                sim_block(b, ORDER, True)
            sim_block(NB - 1, ORDER, True, last=True)
            pool.wait_ge(top_found, T + 2)
            for half in range(2):
                pool.dma_start(hlast[:, half * HBK:(half + 1) * HBK],
                               h_half[2 * NB - 2 + half]).then_inc(hrow_loaded, 16)
            pool.wait_ge(hrow_made, 2 * NB - 1)
            for half in range(2):
                pool.dma_start(hs_half[2 * NB - 2 + half],
                               hlast[:, half * HBK:(half + 1) * HBK]).then_inc(hs_stored, 16)
            pool.wait_ge(hs_stored, 32 * NB)

            def fetch(t, e):
                pool.wait_ge(nbr_scaled, t + 1)
                pool.tensor_copy(idx[:, e], I4[:, bass.ds(t, 1), :].rearrange("p a k -> p (a k)")
                                 ).then_inc(idx_ready, 1)
                pool.wait_ge(idx_ready, t + 1)
                carry_wait(0)
                for k in range(TOP):
                    pool.indirect_dma_start(
                        nbr[:, e * TOP + k], None, hs_dram,
                        bass.IndirectOffsetOnAxis(ap=idx[:, e, k:k + 1], axis=0)).then_inc(nbr_loaded[e], 16)

            def scale(t, qd, e):
                pool.wait_ge(nbr_loaded[e], qd * (16 * TOP) + 16 * TOP)
                pool.wait_ge(nsum_made, t + 1)
                pool.tensor_tensor(nbrs[:, e * TOP:(e + 1) * TOP], nbr[:, e * TOP:(e + 1) * TOP],
                                   S4[:, bass.ds(t, 1), :].rearrange("p a k -> p (a k)").unsqueeze(2)
                                   .to_broadcast([P, TOP, D]), ALU.mult).then_inc(nbr_scaled, 1)

            def quad_neighbours(qd, last=False):
                fetch(qd * 2 + 1, 1)
                scale(qd * 2, qd, 0)
                if not last:
                    fetch(qd * 2 + 2, 0)
                scale(qd * 2 + 1, qd, 1)

            pool.nop().then_inc(nbr_scaled, 2)
            fetch(0, 0)
            load_stage(C_SIM + 1)
            with pool.Fori(0, C_NBR - 1) as c:
                quad_neighbours(c * QUADS)
                load_stage(c + (C_SIM + 2))
                with pool.Fori(1, QUADS) as q:
                    quad_neighbours(c * QUADS + q)
            quad_neighbours((C_NBR - 1) * QUADS)
            load_stage(C_SIM + C_NBR + 1)
            with pool.Fori((C_NBR - 1) * QUADS + 1, C_NBR * QUADS - 1) as qd:
                quad_neighbours(qd)
            quad_neighbours(C_NBR * QUADS - 1, last=True)
            for c in range(C_SIM + C_NBR + 2, C):
                load_stage(c)

            pool.wait_ge(l_ready, ITEM5 + 1)
            for k in range(RING):
                pool.dma_start(xb[:, k * (T // RING):(k + 1) * (T // RING)], x_slot[k]).then_inc(x2_loaded[k], 16)
            pool.dma_start(w2s, W2).then_inc(w2_loaded, 16)
            pool.dma_start(b2bc, b2.partition_broadcast(P)).then_inc(w2_loaded, 16)
            pool.wait_ge(w2_loaded, 32)
            for k in range(RING):
                pool.wait_ge(x2_loaded[k], 16)
            with pool.Fori(0, C // 2) as gg:
                for e in range(2):
                    xg4 = xb[:, bass.ds(gg * (2 * JT) + e * JT, JT), :]
                    pool.tensor_tensor(xg4, xg4, b2bc.unsqueeze(1).to_broadcast([P, JT, D]),
                                       ALU.add).then_inc(xb_made, 1)

        @block.vector
        def _(dve):
            class Steps:
                base, n = 0, 0

            def step(ins):
                Steps.n += 1
                ins.then_inc(dve_step, 1)
                dve.wait_ge(dve_step, Steps.base + Steps.n)

            roots = [0]

            def rsqrt(dst, s, tmp, before):
                dve.reciprocal(tmp, s).then_inc(root_in, 1)
                dve.wait_ge(root_in, before + 1)
                dve.wait_ge(root_out, before + 1)
                newton(dst, s, tmp)

            def newton(dst, s, tmp):
                step(dve.tensor_tensor(tmp, dst, dst, ALU.mult))
                step(dve.tensor_tensor(tmp, tmp, s, ALU.mult))
                step(dve.tensor_scalar(tmp, tmp, -0.5, 1.5, ALU.mult, ALU.add))
                step(dve.tensor_tensor(dst, dst, tmp, ALU.mult))

            def per_row(ap, d):
                return ap.unsqueeze(2).to_broadcast([P, ap.shape[1], d])

            dve.nop().then_inc(acc_added, 2)
            dve.nop().then_inc(l_ready, 1)
            dve.nop().then_inc(z_made, 2)
            dve.nop().then_inc(w_made, 2)
            dve.nop().then_inc(zl_ready, 2)
            dve.nop().then_inc(o_scaled, OB)
            for k in range(RING):
                dve.nop().then_inc(summed[k], 1)
                if shared(SUP - 1, k):
                    dve.nop().then_inc(last_summed[k], first_shared(k) * BODIES + 1)
            for g in range(T // LNG):
                hg, part = h_all[:, g * LNG:(g + 1) * LNG], slice(g * LNG, (g + 1) * LNG)
                dve.wait_ge(x_loaded[g], 16)
                step(dve.reduce_sum(st[:, 0, part], hg, AX_X))
                step(dve.tensor_scalar(st[:, 0, part], st[:, 0, part], 1.0 / D, None, ALU.mult))
                step(dve.tensor_tensor(hg, hg, per_row(st[:, 0, part], D), ALU.subtract))
                step(dve.tensor_tensor(lt, hg, hg, ALU.mult))
                step(dve.reduce_sum(st[:, 1, part], lt, AX_X))
            step(dve.tensor_scalar(st[:, 1], st[:, 1], 1.0 / D, LN_EPS, ALU.mult, ALU.add))
            rsqrt(st[:, 3], st[:, 1], st[:, 2], 0)
            for g in range(T // LNG):
                hg = h_all[:, g * LNG:(g + 1) * LNG]
                step(dve.tensor_tensor(hg, hg, per_row(st[:, 3, g * LNG:(g + 1) * LNG], D), ALU.mult))
                dve.tensor_scalar(hg, hg, 0.0, None, ALU.max).then_inc(h_made, 1)
            step(dve.memset(acc[:, 0:RING * W], 0.0))

            def store_group(s, R):
                dve.wait_ge(m_done, R * (RING * s * JT) + (RING * s * JT + ITEMS1[s] + HB))
                dve.tensor_scalar(acc[:, bass.ds((R + s * RING) * W, W)], ab[0][:, :], 1.0, None,
                                  ALU.mult).then_inc(acc_added, 1)

            def first_rows(s, R, q, store=False):
                item = (R * RING + q) * (s * JT) + ITEMS1[s]
                for what, k in DVE1[s]:
                    if what == "L":
                        jt = k % JT
                        dve.wait_ge(h_ready, item + (k + 1))
                        dve.tensor_tensor(itemL[:, jt], tbank[jt], itemH[:, jt].bitcast(F32),
                                          ALU.subtract).then_inc(l_ready, 1)
                        if k == 0 and store:
                            store_group(s, R - 1)
                    if what == "S":
                        n = JT - 1 if shared(s, k) else JT
                        dve.wait_ge(a_loaded[k], (R * RING + q) * 16 + (s * BODIES * 16 + 16))
                        part = rs_part[:, bass.ds((R + s * RING) * JT, n), bass.ds(q + k * RING, 1)]
                        dve.reduce_sum(part.rearrange("p a b -> p (a b)"), ring[:, k, 0:n],
                                       AX_X).then_inc(summed[k], 1)

            for s in range(SUP):
                if s:
                    with dve.Fori(0, RING) as q:
                        first_rows(s, 0, q)
                    with dve.Fori(1, RING) as R:
                        first_rows(s, R, 0, store=True)
                        with dve.Fori(1, RING) as q:
                            first_rows(s, R, q)
                    store_group(s, RING - 1)
                rows = slice(s * ST, (s + 1) * ST)
                for k in range(RING):
                    dve.wait_ge(summed[k], (s + 1) * BODIES + 1)
                    if shared(s, k):
                        dve.wait_ge(last_summed[k], (s + 1) * BODIES + 1)
                step(dve.reduce_sum(rowsum[:, rows], rs_part[:, rows], AX_X))
                rsqrt(dinv[:, rows], rowsum[:, rows], rt[:, 0, rows], 1 + s)
                dve.wait_ge(h_stored, 16 * (T // LNG))
                dve.wait_ge(h_made, T // LNG)
                for g in range(s * ST // LNG, (s + 1) * ST // LNG):
                    hg = h_all[:, g * LNG:(g + 1) * LNG]
                    step(dve.tensor_tensor(hg, hg, per_row(dinv[:, g * LNG:(g + 1) * LNG], D), ALU.mult))
                dve.nop().then_inc(hs_made, 1)

            def add_group(bank, col, rg, done, sums=None):
                if sums is not None:
                    dve.wait_ge(nsum_added, sums + 2)
                dve.wait_ge(m_done, done + HB)
                dve.wait_ge(acc_added, rg + 2)
                dst = acc[:, bass.ds(col, W)]
                dve.tensor_tensor(dst, dst, ab[bank][:, :], ALU.add).then_inc(acc_added, 1)

            def split_quad(item, rg, col, prev_col, hs_src, nbr_qd=None, beside={}):
                for k in range(QI):
                    dve.wait_ge(h_ready, item + (k + 1))
                    dve.tensor_tensor(itemL[:, k % HB], tbank[k % 4], itemH[:, k % HB].bitcast(F32),
                                      ALU.subtract).then_inc(l_ready, 1)
                    if hs_src is not None and k < JT:
                        dve.wait_ge(hsh_ready, hs_src[1] + (k + 1))
                        dve.tensor_tensor(hsL[:, k], hs_src[0](k), hsH[:, k].bitcast(F32),
                                          ALU.subtract).then_inc(hsl_ready, 1)
                    if k % JT == 2:
                        r = k // JT
                        sums = None if nbr_qd is None else nbr_qd * 2 + int(k > 8)
                        if r:
                            add_group((r - 1) % 2, col + (r - 1) * W, rg + (r - 1), item + r * JT, sums)
                        elif prev_col is not None:
                            add_group((RING - 1) % 2, prev_col, rg - 1, item, sums)
                    if nbr_qd is not None and k in (4, 10):
                        e = int(k == 10)
                        t = nbr_qd * 2 + e
                        dve.wait_ge(nbr_scaled, t + 3)
                        dve.reduce_sum(nsum[:, e], nbrs[:, e * TOP:(e + 1) * TOP].rearrange("p k d -> p d k"),
                                       AX_X).then_inc(nsum_made, 1)
                    if nbr_qd is not None and k in (8, 14):
                        e = int(k == 14)
                        t = nbr_qd * 2 + e
                        dve.wait_ge(nsum_turned, t + 1)
                        dve.wait_ge(acc_added, rg + (3 + 2 * e))
                        dve.wait_ge(nsum_added, t + 2)
                        dst = acc[:, bass.ds(t * P, P)]
                        dve.tensor_tensor(dst, dst, nbank[e], ALU.add).then_inc(nsum_added, 1)
                    if k in beside:
                        beside[k]()

            def chunk(n, quads, rg, item, prev_col, hs_at, hs0, nbrs=False):
                rg, item, hs = n * (quads * RING) + rg, n * (quads * QI) + item, (hs_at, n * JT + hs0)
                split_quad(item, rg, 0, prev_col, hs, n * QUADS - QUADS if nbrs else None)
                if quads > 1:
                    with dve.Fori(1, quads) as q:
                        split_quad(item + q * QI, q * RING + rg, q * (RING * W), q * (RING * W) - W, None,
                                   q + n * QUADS - QUADS if nbrs else None)

            for s in range(SUP):
                run = (s + 1, RG1 + QUADS2[s] * RING, ITEMS1[SUP] + QUADS2[s] * QI)
                last_col = (s + 1) * (RING * W) - W
                hs_at = lambda c, k: h_all[:, bass.ds(c * JT + k, 1), :].rearrange("p a d -> p (a d)")
                hs0 = ITEMS1[SUP] + s * RING * JT
                c = s * RING
                chunk(0, *run, last_col - RING * W if s else None, (lambda k, c=c: hs_at(c, k)), hs0)
                with dve.Fori(1, RING) as n:
                    chunk(n, *run, last_col, lambda k: hs_at(n + s * RING, k), hs0)
            LASTCOL = (C - 1) * W
            add_group((RING - 1) % 2, LASTCOL, RG2 - 1, ITEM2)

            def scale_u(g, e):
                dve.wait_ge(ut_ready, g + 1)
                dve.wait_ge(z_made, g + 1)
                dve.tensor_tensor(wt[:, e].rearrange("p (r d) -> p r d", d=D),
                                  ab[e][:, :].rearrange("p (r d) -> p r d", d=D),
                                  per_row(dinv[:, bass.ds(g * JT, JT)], D), ALU.mult).then_inc(w_made, 1)

            def leaky(g, e):
                dve.wait_ge(b_added, g + 1)
                dve.wait_ge(z_used, g * JT + JT)
                dve.scalar_tensor_tensor(out=zt[:, e], in0=wt[:, e], scalar=SLOPE, in1=wt[:, e],
                                         op0=ALU.mult, op1=ALU.max).then_inc(z_made, 1)

            def low_z(g, e):
                dve.wait_ge(zh_ready, g + 1)
                cols = bass.ds(g * W, W)
                dve.tensor_tensor(zTL[:, cols], tb[e][:, :], zTH[:, cols].bitcast(F32),
                                  ALU.subtract).then_inc(zl_ready, 1)

            pipeline(dve, ((2, scale_u), (1, leaky), (0, low_z)))
            part = [sqp[:, k * T:(k + 1) * T] for k in range(3)]
            dve.wait_ge(z_used, T + 2 * JT)
            step(dve.tensor_copy(part[0], sq[:, :]))
            step(dve.tensor_tensor(sqr, sq[:, :], part[0], ALU.subtract))
            step(dve.tensor_copy(part[1], sqr))
            step(dve.tensor_tensor(sqr, sqr, part[1], ALU.subtract))
            step(dve.tensor_copy(part[2], sqr))
            dve.wait_ge(consts, 1)
            dve.tensor_copy(identb, ident[:, :]).then_inc(sqp_made, 1)
            for k in range(3):
                dve.wait_ge(sqt_ready, k + 1)
                dve.tensor_copy(sqt[0:T, k * P:(k + 1) * P],
                                [tb[0], tb[1], ab[0]][k][0:T, 0:P // 2].bitcast(BF16)).then_inc(sqt_copied, 1)

            dve.wait_ge(acc_cleared, 1)
            dve.nop().then_inc(v_copied, 2)
            dve.nop().then_inc(top_found, 2)

            def sim_tile(b, j, product, last=False):
                t = b * BLK + j

                def add_groups():
                    for r in range(2):
                        g = 2 * j + r
                        add_group(r, g * W, (b - LAG) * C + (RG2 + g), (b - LAG) * ITEMS + (ITEM2 + (g + 1) * JT))

                if product and not last:
                    add_groups()
                dve.wait_ge(v_copied, t * NP + (NP + 2))
                dve.memset(spare[:, 1 + BLK:2 + BLK], 0.0).then_inc(dve_step, 1)
                dve.max(top8[:, j], v[:, j % 2]).then_inc(dve_step, 1)
                Steps.n += 2
                dve.wait_ge(dve_step, Steps.base + Steps.n)
                dve.memset(spare[:, 1 + BLK:2 + BLK], 0.0).then_inc(dve_step, 1)
                Steps.n += 1
                dve.max_index(idx8[:, :], top8[:, j], v[:, j % 2]).then_inc(top_found, 1)
                dve.wait_ge(top_found, t + 3)
                if last:
                    add_groups()
                step(dve.tensor_copy(I4[:, bass.ds(t, 1), :].rearrange("p a k -> p (a k)"), idx8[:, 0:TOP]))

            def distances(b):
                step(dve.tensor_tensor(dist[:, :, :], per_row(sq[:, bass.ds(b * BLK, BLK)], TOP),
                                       top8[:, :, 0:TOP], ALU.subtract))
                dve.tensor_scalar(dist[:, :, :], dist[:, :, :], 0.0, DIST_EPS,
                                  ALU.max, ALU.add).then_inc(dist_made, 1)

            def degrees(b):
                cols = bass.ds(b * BLK, BLK)
                dve.wait_ge(s_made, b + 1)
                step(dve.tensor_copy(S4[:, cols, :], dist[:, :, :]))
                step(dve.reduce_sum(rt[:, 1, 0:BLK], dist[:, :, :], AX_X))
                step(dve.tensor_tensor(rt[:, 1, 0:BLK], rt[:, 1, 0:BLK], rowsum[:, cols], ALU.add))
                dve.reciprocal(rt[:, 0, 0:BLK], rt[:, 1, 0:BLK]).then_inc(root_in, 1)

            def refine(b):
                dve.wait_ge(root_out, b + (ROOTS + 1))
                newton(rt[:, 1, BLK:2 * BLK], rt[:, 1, 0:BLK], rt[:, 0, 0:BLK])
                step(dve.tensor_copy(dinv[:, bass.ds(b * BLK, BLK)], rt[:, 1, BLK:2 * BLK]))

            def scale_hrow(b, half):
                dve.wait_ge(hrow_loaded, b * 32 + (half * 16 + 16))
                dve.tensor_tensor(hrow[:, :, :], hrow[:, :, :],
                                  per_row(dinv[:, bass.ds(b * BLK + half * HBK, HBK)], D),
                                  ALU.mult).then_inc(hrow_made, 1)

            def sim_block(b, product, post, last=False):
                for j in range(BLK):
                    if post and j == 2:
                        degrees(b - 1)
                    if post and j == 4:
                        refine(b - 1)
                        scale_hrow(b - 1, 0)
                    if post and j == 6:
                        scale_hrow(b - 1, 1)
                    sim_tile(b, j, product, last and j == BLK - 1)
                distances(b)

            sim_block(0, False, False)
            sim_block(1, False, True)
            start = Steps.base + Steps.n
            PER = 4 * BLK + 1 + 3 + 5
            with dve.Fori(LAG, NB - 1) as b:
                Steps.base, Steps.n = (b - LAG) * PER + start, 0
                sim_block(b, True, True)
                assert Steps.n == PER
            Steps.base, Steps.n = start + (NB - 1 - LAG) * PER, 0
            sim_block(NB - 1, True, True, last=True)

            def scale_hlast():
                dve.wait_ge(hrow_loaded, 32 * NB)
                dve.tensor_tensor(hlast, hlast, per_row(dinv[:, T - BLK:T], D), ALU.mult).then_inc(hrow_made, 1)

            def finish_degrees():
                refine(NB - 1)
                scale_hlast()

            dve.nop().then_inc(nsum_made, 2)
            dve.nop().then_inc(nsum_added, 2)
            hs_at = lambda k: hs_stage[:, k]
            hs5 = HS2 + C_SIM * JT
            for q in range(QUADS):
                split_quad(ITEM5 + q * QI, RG5 + q * RING, q * RING * W, q * RING * W - W if q else None,
                           None if q else (hs_at, hs5),
                           beside={0: {QI - 1: lambda: degrees(NB - 1)}, 1: {QI - 1: finish_degrees}}.get(q, {}))
            with dve.Fori(1, 1 + C_NBR) as n:
                chunk(n, QUADS, RG5, ITEM5, LASTCOL, hs_at, hs5, nbrs=True)
            with dve.Fori(1 + C_NBR, C - C_SIM) as n:
                chunk(n, QUADS, RG5, ITEM5, LASTCOL, hs_at, hs5)
            add_group((RING - 1) % 2, LASTCOL, RG2 + C * C - 1, 2 * ITEM2)

            with dve.Fori(0, C // OB) as gg:
                for e in range(OB):
                    g = gg * OB + e
                    o3 = ot[:, e]
                    dve.wait_ge(o_ready, g + 3)
                    dve.wait_ge(out_stored[e], gg * 16 + 16)
                    dve.tensor_tensor(o3, obank[e].rearrange("p (r d) -> p r d", d=D),
                                      per_row(dinv[:, bass.ds(g * JT, JT)], D), ALU.mult).then_inc(o_scaled, 1)
                    dve.wait_ge(o_scaled, g + (1 + OB))
                    dve.wait_ge(xb_made, g + 1)
                    dve.tensor_tensor(o3, o3, xb[:, bass.ds(g * JT, JT), :], ALU.add).then_inc(o_made, 1)

        @block.tensor
        def _(pe):
            pe.nop().then_inc(t_ready, TR)
            pe.nop().then_inc(o_ready, 2)
            pe.nop().then_inc(m_done, HB)
            pe.wait_ge(consts, 1)

            def first_turn(s, m, item, body):
                k, jt = (m // JT) % s, m % JT
                if jt == 0:
                    pe.wait_ge(a_loaded[k], body * 16 + (16 * (m // (s * JT)) + s * BODIES * 16 + 16))
                if not isinstance(item, int) or item + m > 2:
                    pe.wait_ge(l_ready, item + (m - 2))
                for r in range(JT):
                    last = pe.transpose(tbank[jt][:, r * P:(r + 1) * P],
                                        ring[:, k, r, jt * P:(jt + 1) * P], ident[:, :])
                last.then_inc(t_ready, 1)

            def first_body(s, R, q, start=False, stop=False, last=False):
                body = R * RING + q
                item = body * (s * JT) + ITEMS1[s]
                for m in range(s * JT):
                    jt = m % JT
                    if not (last and m + LEAD >= s * JT):
                        first_turn(s, m + LEAD, item, body)
                    pe.wait_ge(l_ready, item + (m + 2))
                    if start and m == 0:
                        pe.wait_ge(acc_added, R + ((s - 1) * RING + 2))
                    pe.wait_ge(hsl_ready, item + (m + 1))
                    H, L, dst = itemH[:, jt], itemL[:, jt], ab[0][:, :]
                    pe.matmul(dst, hsH[:, jt], H, start=start and m == 0, stop=False)
                    pe.matmul(dst, hsH[:, jt], L, start=False, stop=False)
                    pe.matmul(dst, hsL[:, jt], H, start=False,
                              stop=stop and m == s * JT - 1).then_inc(m_done, 1)

            for s in range(1, SUP):
                for m in range(LEAD):
                    first_turn(s, m, ITEMS1[s], 0)
                with pe.Fori(0, RING - 1) as R:
                    first_body(s, R, 0, start=True)
                    with pe.Fori(1, RING - 1) as q:
                        first_body(s, R, q)
                    first_body(s, R, RING - 1, stop=True)
                first_body(s, RING - 1, 0, start=True)
                with pe.Fori(1, RING - 1) as q:
                    first_body(s, RING - 1, q)
                first_body(s, RING - 1, RING - 1, stop=True, last=True)
            pe.wait_ge(acc_added, RG1 + 2)

            def turn(k, item, quads, free=True):
                slot, jt = (k // JT) % RING, k % JT
                if jt == 0:
                    pe.wait_ge(a_loaded[slot], quads * 16 + (16 * (k // QI) + 16))
                if free:
                    pe.wait_ge(l_ready, item + (k - 2))
                for r in range(JT):
                    last = pe.transpose(tbank[k % 4][:, r * P:(r + 1) * P],
                                        ring[:, slot, r, jt * P:(jt + 1) * P], ident[:, :])
                last.then_inc(t_ready, 1)

            def multiply(k, item, rg, hs_count):
                jt, bank = k % JT, (k // JT) % 2
                pe.wait_ge(l_ready, item + (k + 2))
                pe.wait_ge(h_ready, item + k + 1)
                if jt == 0:
                    pe.wait_ge(acc_added, rg + (k // JT + 1))
                if hs_count is not None:
                    pe.wait_ge(hsl_ready, hs_count + jt + 1)
                dst = ab[bank][:, :]
                H, L = itemH[:, k % HB], itemL[:, k % HB]
                pe.matmul(dst, hsH[:, jt], H, start=jt == 0, stop=False)
                pe.matmul(dst, hsH[:, jt], L, start=False, stop=False)
                pe.matmul(dst, hsL[:, jt], H, start=False, stop=jt == JT - 1).then_inc(m_done, 1)

            def quad(item, rg, quads, hs_count, last=False, nbr=None):
                for k in range(QI):
                    if k + LEAD < QI or not last:
                        turn(k + LEAD, item, quads)
                    multiply(k, item, rg, hs_count if k < JT else None)
                    if nbr is not None and k in (6, 12):
                        e = int(k == 12)
                        pe.wait_ge(nsum_made, nbr * 2 + (e + 3))
                        pe.wait_ge(nsum_added, nbr * 2 + (e + 1))
                        pe.transpose(nbank[e], nsum[:, e], ident[:, :]).then_inc(nsum_turned, 1)

            def product(runs, nbrs_of=0):
                for k in range(LEAD):
                    turn(k, runs[0][2], runs[0][4], free=False)
                for i, (n, quads, item0, rg0, load0, hs0, nbrs) in enumerate(runs):
                    def chunk(c, stop):
                        with pe.Fori(0, stop) as q:
                            quad(c * (quads * QI) + q * QI + item0, c * (quads * RING) + q * RING + rg0,
                                 c * quads + q + load0, c * JT + hs0, nbr=c * quads + q if nbrs else None)

                    end = i == len(runs) - 1
                    if n > end:
                        with pe.Fori(0, n - end) as c:
                            chunk(c, quads)
                    if end:
                        chunk(n - 1, quads - 1)
                        quad((n * quads - 1) * QI + item0, (n * quads - 1) * RING + rg0,
                             n * quads - 1 + load0, (n - 1) * JT + hs0, last=True)

            product([(RING, s + 1, ITEMS1[SUP] + QUADS2[s] * QI, RG1 + QUADS2[s] * RING,
                      SUP * BODIES + QUADS2[s], ITEMS1[SUP] + s * RING * JT, False) for s in range(SUP)])

            pe.wait_ge(acc_added, RG2 + 2)
            pe.wait_ge(w_loaded, 32)
            pe.wait_ge(l_ready, ITEM2 + 1)
            def times_w1(g, e):
                pe.wait_ge(us_ready, g + 1)
                pe.matmul(tbank[2 + e], w1s, acc[:, bass.ds(g * W, W)], start=True, stop=True).then_inc(u_ready, 1)

            def turn_u(g, e):
                pe.wait_ge(us_ready, g + 3)
                pe.wait_ge(w_made, g + 1)
                for r in range(JT):
                    last = pe.transpose(ab[e][:, r * P:(r + 1) * P], us[:, e, r * P:(r + 1) * P], ident[:, :])
                last.then_inc(ut_ready, 1)

            def turn_z(g, e):
                pe.wait_ge(z_made, g + 3)
                pe.wait_ge(zl_ready, g + 1)
                for r in range(JT):
                    last = pe.transpose(tb[e][:, r * P:(r + 1) * P], zt[:, e, r * P:(r + 1) * P], ident[:, :])
                last.then_inc(zt_ready, 1)

            pipeline(pe, ((3, times_w1), (2, turn_u), (0, turn_z)))
            pe.wait_ge(sqp_made, 1)
            pe.wait_ge(zl_ready, C + 2)
            for k in range(3):
                pe.transpose([tb[0], tb[1], ab[0]][k][0:T, 0:P // 2].bitcast(BF16), sqp[:, k * T:(k + 1) * T],
                             identb).then_inc(sqt_ready, 1)

            pe.wait_ge(sqt_copied, 3)
            pe.wait_ge(sq_loaded, 64)
            pe.wait_ge(zh_ready, C)

            def sim_tile(b, j, par, order):
                t = b * BLK + j
                if len(order) > len(SIM_ONLY):
                    item, rg = (b - LAG) * ITEMS + (j * (2 * JT) + ITEM2), (b - LAG) * C + (j * 2 + RG2)
                pe.wait_ge(z2_ready, t * 2 + 2)
                for what, k in order:
                    if what == "T":
                        half, jt = (k // 2) % 2, k % 2
                        if jt == 0:
                            pe.wait_ge(ah_loaded[half], (b - LAG) * (16 * C) + (j * 32 + (16 * (k // JT) + 16)))
                        pe.wait_ge(t_copied, item + (k + 1 - ITEM2))
                        for r in range(JT):
                            last = pe.transpose(tb[k % 2][:, r * P:(r + 1) * P],
                                                ringh[:, half * JT + r, jt * P:(jt + 1) * P], ident[:, :])
                        last.then_inc(t_ready, 1)
                    if what == "M":
                        multiply(k, item, rg, (b - LAG) * JT + HS2)
                    if what == "Z":
                        pr, q = k // 2, k // 4
                        if k % 2 == 0:
                            pe.wait_ge(v_copied, t * NP + pr + 1)
                        dst = zz[pr % 2][:, (k % 2) * W:(k % 2 + 1) * W]
                        cols = slice(k * W, (k + 1) * W)
                        pe.matmul(dst, z2H[:, par], zTH[:, cols], start=True, stop=False)
                        pe.matmul(dst, z2H[:, par], zTL[:, cols], start=False, stop=False)
                        pe.matmul(dst, z2L[:, par], zTH[:, cols], start=False, stop=False)
                        last = pe.matmul(dst, negones[32 * q:32 * q + 3, :],
                                         sqrow[32 * q:32 * q + 3, (k % 4) * W:(k % 4 + 1) * W],
                                         start=False, stop=True)
                        if k % 2:
                            last.then_inc(zz_ready, 1)

            for b in range(LAG):
                with pe.Fori(0, BLK // 2) as pair:
                    for par in range(2):
                        sim_tile(b, pair * 2 + par, par, SIM_ONLY)
            with pe.Fori(LAG, NB - 1) as b:
                with pe.Fori(0, BLK // 2) as pair:
                    for par in range(2):
                        sim_tile(b, pair * 2 + par, par, ORDER)
            with pe.Fori(0, BLK // 2 - 1) as pair:
                for par in range(2):
                    sim_tile(NB - 1, pair * 2 + par, par, ORDER)
            sim_tile(NB - 1, BLK - 2, 0, ORDER)
            sim_tile(NB - 1, BLK - 1, 1, LAST_ORDER)

            pe.wait_ge(v_copied, T * NP + 2)
            pe.wait_ge(t_copied, C_SIM * ITEMS + 2)
            pe.wait_ge(l_ready, ITEM5 + 1)
            product([(n, QUADS, ITEM5 + c * ITEMS, RG5 + c * C, QUAD5 + c * QUADS, HS2 + (C_SIM + c) * JT, nbrs)
                     for c, n, nbrs in ((0, 1, False), (1, C_NBR, True), (1 + C_NBR, C - C_SIM - C_NBR - 1, False))])

            pe.wait_ge(acc_added, RG2 + C * C + 2)
            pe.wait_ge(w2_loaded, 32)
            with pe.Fori(0, C // OB) as gg:
                for e in range(OB):
                    g = gg * OB + e
                    pe.wait_ge(accs_ready, g + 1)
                    pe.wait_ge(o_scaled, g + 1)
                    for r in range(JT):
                        last = pe.matmul(obank[e][:, r * P:(r + 1) * P], accs[:, e % 2, r * P:(r + 1) * P], w2s,
                                         start=True, stop=True)
                    last.then_inc(o_ready, 1)


_INS = ["x", "adj", "L0_gnn_W1", "L0_gnn_b1", "L0_gnn_W2", "L0_gnn_b2"]


def kernel(**inputs):
    import numpy as np
    import concourse.bacc as bacc
    from concourse.bass_utils import run_bass_kernel_spmd

    nc = bacc.Bacc("TRN2", target_bir_lowering=False, num_devices=1)
    arrays, args = {}, []
    for name in _INS:
        a = np.ascontiguousarray(inputs[name])
        arrays[name + "_in"] = a
        args.append(nc.dram_tensor(name + "_in", a.shape, mybir.dt.from_np(a.dtype), kind="ExternalInput").ap())
    out = nc.dram_tensor("out", inputs["x"].shape, F32, kind="ExternalOutput").ap()
    gnn_kernel(nc, *args, out)
    r = run_bass_kernel_spmd(nc, [arrays], core_ids=[0])
    return r.results[0]["out"]
```
